# Optimizing a Trainium2 kernel written in Bass

```python
import numpy as np
import jax
import jax.numpy as jnp

def _softmax(x, axis=-1):
    return jax.nn.softmax(x, axis=axis)

def _gelu(x):
    return jax.nn.gelu(x, approximate=True)

def _silu(x):
    return jax.nn.silu(x)

def _sigmoid(x):
    return jax.nn.sigmoid(x)

def _layernorm(x, axis=-1, eps=1e-05):
    m = jnp.mean(x, axis=axis, keepdims=True)
    v = jnp.var(x, axis=axis, keepdims=True)
    return (x - m) / jnp.sqrt(v + eps)

def _scatter_add(tgt, idx, src, axis=0):
    return tgt.at[idx].add(src)

def _segment_sum(src, seg, n):
    return jax.ops.segment_sum(src, seg, n)
kernel_name = 'mk_prb_d1_jaxref_r8_7be27f'

def setup_inputs(seed: int=0):
    np.random.seed(seed)
    _w = jnp.asarray

    def _L0_attn_setup():
        import jax, jax.numpy as jnp
        import numpy as np
        N, L, D_IN, H, HD, D_OUT = (4, 256, 128, 16, 64, 128)
        DIM = H * HD
        key = jax.random.key(seed)
        ks = jax.random.split(key, 5)
        s_in = 1.0 / np.sqrt(D_IN)
        s_d = 1.0 / np.sqrt(DIM)
        return {'data': jax.random.normal(ks[0], (N, L, D_IN), jnp.float32), 'W_qkv': jax.random.uniform(ks[1], (D_IN, 3 * DIM), jnp.float32, -s_in, s_in), 'b_qkv': jax.random.uniform(ks[2], (3 * DIM,), jnp.float32, -s_in, s_in), 'W_out': jax.random.uniform(ks[3], (DIM, D_OUT), jnp.float32, -s_d, s_d), 'b_out': jax.random.uniform(ks[4], (D_OUT,), jnp.float32, -s_d, s_d)}
    _L0_attn_in = _L0_attn_setup()

    def _L0_ffn_setup():
        import jax, jax.numpy as jnp
        import numpy as np
        from jax import lax
        T, B, I, M, O = (32, 64, 128, 128, 128)

        def _xavier(key, shape):
            fan_out, fan_in = shape
            limit = float(np.sqrt(6.0 / (fan_in + fan_out)))
            return jax.random.uniform(key, shape, jnp.float32, -limit, limit)
        key = jax.random.key(seed)
        ks = jax.random.split(key, 9)
        x = jax.random.normal(ks[0], (T, B, I), jnp.float32)
        return {'x': x, 'wf': _xavier(ks[1], (M, I)), 'uf': _xavier(ks[2], (M, M)), 'bf': jnp.zeros((M,), jnp.float32), 'wi': _xavier(ks[3], (M, I)), 'ui': _xavier(ks[4], (M, M)), 'bi': jnp.zeros((M,), jnp.float32), 'wc': _xavier(ks[5], (M, I)), 'uc': _xavier(ks[6], (M, M)), 'bc': jnp.zeros((M,), jnp.float32), 'wo': _xavier(ks[7], (O, I)), 'uo': _xavier(ks[8], (O, M)), 'bo': jnp.zeros((O,), jnp.float32), 'in_c': jnp.zeros((M,), jnp.float32)}
    _L0_ffn_in = _L0_ffn_setup()
    _d = {'L0_attn_data': _L0_attn_in['data'], 'L0_attn_W_qkv': _L0_attn_in['W_qkv'], 'L0_attn_b_qkv': _L0_attn_in['b_qkv'], 'L0_attn_W_out': _L0_attn_in['W_out'], 'L0_attn_b_out': _L0_attn_in['b_out'], 'L0_ffn_wf': _L0_ffn_in['wf'], 'L0_ffn_uf': _L0_ffn_in['uf'], 'L0_ffn_bf': _L0_ffn_in['bf'], 'L0_ffn_wi': _L0_ffn_in['wi'], 'L0_ffn_ui': _L0_ffn_in['ui'], 'L0_ffn_bi': _L0_ffn_in['bi'], 'L0_ffn_wc': _L0_ffn_in['wc'], 'L0_ffn_uc': _L0_ffn_in['uc'], 'L0_ffn_bc': _L0_ffn_in['bc'], 'L0_ffn_wo': _L0_ffn_in['wo'], 'L0_ffn_uo': _L0_ffn_in['uo'], 'L0_ffn_bo': _L0_ffn_in['bo'], 'L0_ffn_in_c': _L0_ffn_in['in_c']}
    _x0 = _d['L0_attn_data']
    _d['L0_attn_data'] = jax.random.normal(jax.random.fold_in(jax.random.key(seed), 1), (8, 512, 128), dtype=_x0.dtype)
    del _x0
    return _d

def reference(L0_attn_data, L0_attn_W_qkv, L0_attn_b_qkv, L0_attn_W_out, L0_attn_b_out, L0_ffn_wf, L0_ffn_uf, L0_ffn_bf, L0_ffn_wi, L0_ffn_ui, L0_ffn_bi, L0_ffn_wc, L0_ffn_uc, L0_ffn_bc, L0_ffn_wo, L0_ffn_uo, L0_ffn_bo, L0_ffn_in_c):

    def _L0_attn_ref(data, W_qkv, b_qkv, W_out, b_out):
        import jax, jax.numpy as jnp
        import numpy as np
        N, L, D_IN, H, HD, D_OUT = (4, 256, 128, 16, 64, 128)
        DIM = H * HD
        n, l = (data.shape[0], data.shape[1])
        qkv = data @ W_qkv + b_qkv
        q = qkv[:, :, :DIM].reshape(n, l, H, HD)
        k = qkv[:, :, DIM:2 * DIM].reshape(n, l, H, HD)
        v = qkv[:, :, 2 * DIM:].reshape(n, l, H, HD)
        scores = jnp.einsum('nqhd,nkhd->nhqk', q, k)
        attention = jax.nn.softmax(scores / jnp.sqrt(jnp.float32(HD)), axis=3)
        out = jnp.einsum('nhql,nlhd->nqhd', attention, v).reshape(n, l, DIM)
        return out @ W_out + b_out

    def _L0_ffn_ref(x, wf, uf, bf, wi, ui, bi, wc, uc, bc, wo, uo, bo, in_c):
        import jax, jax.numpy as jnp
        import numpy as np
        from jax import lax
        T, B, I, M, O = (32, 64, 128, 128, 128)

        def _xavier(key, shape):
            fan_out, fan_in = shape
            limit = float(np.sqrt(6.0 / (fan_in + fan_out)))
            return jax.random.uniform(key, shape, jnp.float32, -limit, limit)
        batch = x.shape[1]
        c0 = jnp.broadcast_to(in_c, (batch, in_c.shape[0]))

        def step(c, xt):
            ft = jax.nn.sigmoid(xt @ wf.T + c @ uf.T + bf)
            it = jax.nn.sigmoid(xt @ wi.T + c @ ui.T + bi)
            gt = jnp.tanh(xt @ wc.T + c @ uc.T + bc)
            c = ft * c + it * gt
            return (c, None)
        c_final, _ = lax.scan(step, c0, x)
        h = jnp.tanh(jnp.einsum('tbi,oi->tbo', x, wo) + c_final @ uo.T + bo)
        return h
    x = L0_attn_data
    xn = _layernorm(x, axis=-1)
    x = x + _L0_attn_ref(xn, L0_attn_W_qkv, L0_attn_b_qkv, L0_attn_W_out, L0_attn_b_out) + _L0_ffn_ref(xn, L0_ffn_wf, L0_ffn_uf, L0_ffn_bf, L0_ffn_wi, L0_ffn_ui, L0_ffn_bi, L0_ffn_wc, L0_ffn_uc, L0_ffn_bc, L0_ffn_wo, L0_ffn_uo, L0_ffn_bo, L0_ffn_in_c)
    return x

_drawn_inputs = setup_inputs


def setup_inputs(seed=0):
    import zlib

    import numpy as np

    out = dict(_drawn_inputs(seed))
    spreads = {'L0_ffn_bf': (0.0, 0.736),
     'L0_ffn_bi': (0.0, 0.698),
     'L0_ffn_bc': (0.0, 0.1),
     'L0_ffn_bo': (0.0, 0.1),
     'L0_ffn_in_c': (0.0, 0.8)}
    factors = {'L0_attn_W_qkv': 3.775, 'L0_attn_b_out': 3.666}
    for name, (base, spread) in spreads.items():
        noise = np.random.default_rng([zlib.crc32(name.encode()), seed]).standard_normal(out[name].shape)
        drawn = base * np.exp(spread * noise) if base else spread * noise
        out[name] = jnp.asarray(drawn.astype(out[name].dtype))
    for name, factor in factors.items():
        out[name] = (out[name] * factor).astype(out[name].dtype)
    return out
```

```python
import concourse.bass as bass
from concourse import mybir
from contextlib import ExitStack


def build_block(nc, data, W_qkv, b_qkv, W_out, b_out, wf, uf, bf, wi, ui, bi, wc, uc, bc, wo, uo, bo, in_c, out):
    f32 = mybir.dt.float32
    f32r = mybir.dt.float32r
    ALU = mybir.AluOpType
    ACT = mybir.ActivationFunctionType
    AX = mybir.AxisListType

    P = 128
    N, L, D = data.shape
    DIM = W_qkv.shape[1] // 3
    PAIRS = DIM // P
    HD = P // 2
    TB = L // P
    SCALE = float(HD) ** -0.5
    EPS = 1e-5
    HALVES = 2
    BIASES = 3 * PAIRS + 6
    B_V, B_OUT, B_F, B_I, B_C, B_O, IN_C = 2 * PAIRS, 3 * PAIRS, 25, 26, 27, 28, 29
    OWN = [slice(0, HD), slice(HD, P)]
    OTHER = [slice(HD, P), slice(0, HD)]
    AUX = [slice(HD, HD + 1), slice(0, 1)]

    data_t = data.rearrange("n (b p) d -> p n b d", p=P)
    out_t = out.rearrange("n (b p) d -> p n b d", p=P)
    Wo_v = W_out.rearrange("(c p) d -> p c d", p=P)

    ctx = ExitStack()
    with ctx:
        def sb(name, shape, dt=f32):
            return ctx.enter_context(nc.sbuf_tensor(name, shape, dt))

        def sem(name):
            return ctx.enter_context(nc.semaphore(name))

        ident = sb("ident", [P, P])
        ones = sb("ones", [P, HD])
        brow = sb("brow", [32, P])
        bcol = sb("bcol", [P, 32])
        bhalf = sb("bhalf", [P, 2])
        bfin = sb("bfin", [P, 1])
        probs = sb("probs", [P, 2, 2, TB, L])
        XH = sb("XH", [P, N, L], f32r)
        XL = sb("XL", [P, N, L], f32r)
        WH = sb("WH", [P, 3 * DIM], f32r)
        WL = sb("WL", [P, 3 * DIM], f32r)
        WO = sb("WO", [P, PAIRS, D])
        VALL = sb("VALL", [P, TB, DIM])
        XSH = sb("XSH", [P, L], f32r)
        XSL = sb("XSL", [P, L], f32r)
        VS = sb("VS", [P, 2, TB, P])
        Q32 = sb("Q32", [P, 2, L])
        K32 = sb("K32", [P, L])
        QB = sb("QB", [P, 4, 2, L], f32r)
        KA = sb("KA", [P, 4, 2, L], f32r)
        QC = sb("QC", [P, 2, 2, L], f32r)
        KC = sb("KC", [P, 2, 2, L], f32r)
        PSUMK = sb("PSUMK", [P, 2, L])
        PVR = sb("PVR", [P, L])
        DT = sb("DT", [P, L])
        R16 = sb("R16", [P, L // 32])
        RD = sb("RD", [P, L])
        AT = sb("AT", [P, PAIRS, L])
        OT = sb("OT", [P, L])
        RES = sb("RES", [P, TB, D])
        OUTB = sb("OUTB", [P, TB, D])
        NM = sb("NM", [P, 2, 32])
        TM = sb("TM", [P, 2, 2 * 32])
        stats = sb("stats", [P, 2 * TB, 6])
        mv = sb("mv", [P, 2, TB, 2])
        rstd = sb("rstd", [P, 2, TB])
        std = sb("std", [P, 2, TB])
        epst = sb("epst", [P, 1])

        x_all = probs[:, 0, :, :, :].rearrange("p a b l -> p (a b l)").rearrange("p (n b d) -> p n b d", n=N, d=D)
        rest = probs[:, 1, :, :, :].rearrange("p a b l -> p (a b l)")
        W_raw = rest[:, 0:3 * DIM]
        w_raw = rest[:, 3 * DIM:3 * DIM + 8 * P].rearrange("p (w i) -> p w i", w=8)
        xn = AT[:, 0:2, :].rearrange("p a (b d) -> p a b d", d=D)
        tf, ti, tg = AT[:, 2, :], AT[:, 3, :], AT[:, 4, :]
        Dst = AT[:, 5, :]
        Abuf, Bbuf = AT[:, 6, :], AT[:, 7, :]
        HT = [tf, ti]
        rsum = VALL[:, :, :].rearrange("p b c -> p (b c)").rearrange("p (n b d) -> p n b d", n=N, d=D)
        gwH = QB[:, 0, :, :].rearrange("p a (w m) -> p (a w) m", m=P)
        gwL = KA[:, 0, :, :].rearrange("p a (w m) -> p (a w) m", m=P)
        DH, DL = QB[:, 1, 0, :], KA[:, 1, 0, :]

        st = ctx.enter_context(nc.psum_tensor("st", [P, 2, 2, L], f32))
        mx = ctx.enter_context(nc.psum_tensor("mx", [P, 2, L], f32))
        pv = ctx.enter_context(nc.psum_tensor("pv", [P, L], f32))
        misc = ctx.enter_context(nc.psum_tensor("misc", [P, L], f32))
        gate = [[st[:, 0, 0, :], st[:, 0, 1, :], mx[:, 0, :]], [st[:, 1, 0, :], st[:, 1, 1, :], mx[:, 1, :]]]

        passed_sp, passed_dve = sem("passed_sp"), sem("passed_dve")
        ld_b, ld_x, ld_w, ld_W, ld_wo = sem("ld_b"), sem("ld_x"), sem("ld_w"), sem("ld_W"), sem("ld_wo")
        id0, id1, ones_set, pads_set, eps_set = sem("id0"), sem("id1"), sem("ones_set"), sem("pads_set"), sem("eps_set")
        bias_tr, bias_col, bias_half, bias_fold, bias_fin = (sem("bias_tr"), sem("bias_col"), sem("bias_half"),
                                                             sem("bias_fold"), sem("bias_fin"))
        gw_tr, gw_hi, gw_lo = sem("gw_tr"), sem("gw_hi"), sem("gw_lo")
        bn_part, bn_done, std_done, rstd_done, xn_done, xt_done, xh_done, xl_done = (
            sem("bn_part"), sem("bn_done"), sem("std_done"), sem("rstd_done"), sem("xn_done"), sem("xt_done"),
            sem("xh_done"), sem("xl_done"))
        wh_done, wl_done = sem("wh_done"), sem("wl_done")
        state, state_hi, state_lo, gates_done, t_done, ab_done = (
            sem("state"), sem("state_hi"), sem("state_lo"), sem("gates_done"), sem("t_done"), sem("ab_done"))
        h_done, ht_done, htr_done, r_done, out_rows = (sem("h_done"), sem("ht_done"), sem("htr_done"), sem("r_done"),
                                                    sem("out_rows"))
        q_done, k_done, v_done, den_done, o_done, tr_done = (
            sem("q_done"), sem("k_done"), sem("v_done"), sem("den_done"), sem("o_done"), sem("tr_done"))
        st_done, mx_done, pv_done = sem("st_done"), sem("mx_done"), sem("pv_done")
        q_evac, k_evac, v_evac, q_hi, k_hi, exp_done, pv_evac, o_evac = (
            sem("q_evac"), sem("k_evac"), sem("v_evac"), sem("q_hi"), sem("k_hi"), sem("exp_done"),
            sem("pv_evac"), sem("o_evac"))
        q_lo, k_lo, red_done, tm_done, den_used, r16_done, rd_done, out_done = (
            sem("q_lo"), sem("k_lo"), sem("red_done"), sem("tm_done"), sem("den_used"), sem("r16_done"),
            sem("rd_done"), sem("out_done"))
        sum_part, sum_done, norm_done = sem("sum_part"), sem("sum_done"), sem("norm_done")
        d_dup = [sem("d_dup0"), sem("d_dup1")]
        d_kc = [sem("d_kc0"), sem("d_kc1")]
        d_m = [sem("d_m0"), sem("d_m1")]
        d_vs = [sem("d_vs0"), sem("d_vs1")]
        d_xs, d_res = sem("d_xs"), sem("d_res")

        def wait(eng, s, value):
            if not (isinstance(value, int) and value <= 0):
                eng.wait_ge(s, value)

        def dmas(n, s, each):
            return (4 * n + s // 2 + 1) * (16 * each)

        def batches(eng, step):
            step(0, True, False)
            with eng.Fori(1, N - 1) as n:
                step(n, False, False)
            step(N - 1, False, True)

        block = ctx.enter_context(nc.Block())

        @block.sync
        def _(sp):
            sp.dma_start(brow[0:3 * PAIRS, :], b_qkv.rearrange("(c r) -> c r", r=P)).then_inc(ld_b, 16)
            for i, v in enumerate((b_out, bf, bi, bc, bo, in_c)):
                sp.dma_start(brow[B_OUT + i:B_OUT + i + 1, :], v.rearrange("(a r) -> a r", a=1)).then_inc(ld_b, 16)
            for n in range(0, N, 2):
                sp.dma_start(x_all[:, n:n + 2, :, :], data_t[:, n:n + 2, :, :]).then_inc(ld_x, 16)
                sp.wait_ge(ld_x, 8 * n + 16)
                sp.sem_inc(passed_sp, 1)
            for i, w in enumerate((wf, wi, wc, wo, uf, ui, uc, uo)):
                sp.dma_start(w_raw[:, i, :], w).then_inc(ld_w, 16)
            sp.dma_start(W_raw, W_qkv).then_inc(ld_W, 16)
            sp.dma_start(WO[:, :, :], Wo_v).then_inc(ld_wo, 16)
            with sp.Fori(0, N // 2) as m:
                for k in range(2):
                    sp.wait_ge(r_done, 2 * m + k + 1)
                    sp.sem_inc(passed_sp, 1)
                    sp.dma_start(out_t[:, 2 * m + k, :, :],
                                 rsum[:, 2 * m + k, :, :]).then_inc(out_rows, 16)

            def stage_x(n):
                sp.wait_ge(xl_done, N)
                sp.dma_start(XSH[:, :].bitcast(f32), XH[:, n, :].bitcast(f32)).then_inc(d_xs, 16)
                sp.dma_start(XSL[:, :].bitcast(f32), XL[:, n, :].bitcast(f32)).then_inc(d_xs, 16)

            def duplicate_q(n, s):
                t = 8 * n + s
                sp.wait_ge(q_hi, 2 * t + 2)
                sp.sem_inc(passed_sp, 1)
                for h in range(2):
                    sp.dma_start(QB[OTHER[h], s % 4, h, :].bitcast(f32), QB[OWN[h], s % 4, h, :].bitcast(f32)).then_inc(d_dup[s % 2], 16)

            def copy_k(n, s):
                t = 8 * n + s
                wait(sp, st_done, 4 * t - 4)
                sp.sem_inc(passed_sp, 1)
                sp.wait_ge(k_hi, 2 * t + 2)
                sp.sem_inc(passed_sp, 1)
                for h in range(2):
                    sp.dma_start(KC[OWN[h], s % 2, h, :].bitcast(f32), KA[OWN[h], s % 4, h, :].bitcast(f32)).then_inc(d_kc[s % 2], 16)

            def place_max(n, s):
                t = 8 * n + s
                sp.wait_ge(tm_done, t + 1)
                sp.sem_inc(passed_sp, 1)
                for h in range(2):
                    for b in range(4):
                        dst = QC[AUX[h], s % 2, h, :].bitcast(f32).rearrange("p (q b j) -> p q b j", b=4, j=32)
                        sp.dma_start(dst[:, :, b, :],
                                     TM[32 * b:32 * b + 4, s % 2, 32 * h:32 * h + 32]
                                     ).then_inc(d_m[s % 2], 16)

            stage_x(0)
            sp.wait_ge(pads_set, 6)
            duplicate_q(0, 0)
            copy_k(0, 0)
            duplicate_q(0, 1)
            place_max(0, 0)

            def step(n, first, last):
                for s in range(PAIRS):
                    t = 8 * n + s
                    if not (last and s == 7):
                        copy_k(n, s + 1)
                    sp.wait_ge(v_evac, 8 * n + (4 if s < 4 else 8))
                    sp.sem_inc(passed_sp, 1)
                    wait(sp, pv_done, t - 1)
                    sp.sem_inc(passed_sp, 1)
                    sp.dma_start(VS[:, s % 2, :, :], VALL[:, :, s * P:(s + 1) * P]).then_inc(d_vs[s % 2], 16)
                    if s == 0 and not first:
                        sp.wait_ge(out_rows, 16 * N)
                        sp.dma_start(RES[:, :, :], out_t[:, n - 1, :, :]).then_inc(d_res, 16)
                    if s == 3 and not first:
                        sp.wait_ge(out_done, n)
                        sp.sem_inc(passed_sp, 1)
                        sp.dma_start(out_t[:, n - 1, :, :], OUTB[:, :, :]).then_inc(out_rows, 16)
                    if s == 4 and not last:
                        sp.wait_ge(v_done, 8 * n + 8)
                        sp.sem_inc(passed_sp, 1)
                        stage_x(n + 1)
                    if not (last and s >= 6):
                        duplicate_q(n, s + 2)
                    if not (last and s == 7):
                        place_max(n, s + 1)

            batches(sp, step)
            sp.wait_ge(out_done, N - 1)
            sp.dma_start(RES[:, :, :], out_t[:, N - 1, :, :]).then_inc(d_res, 16)
            sp.wait_ge(out_done, N)
            sp.dma_start(out_t[:, N - 1, :, :], OUTB[:, :, :]).then_inc(out_rows, 16)
            sp.wait_ge(out_rows, 16 * 2 * N)

        @block.gpsimd
        def _(pool):
            nc.gpsimd.memset(ident[:, :], 0.0).then_inc(id0, 1)
            pool.wait_ge(id0, 1)
            nc.gpsimd.affine_select(out=ident[:, :], in_=ident[:, :], compare_op=ALU.not_equal, fill=1.0, base=0,
                                    pattern=[[-1, P]], channel_multiplier=1).then_inc(id1, 1)
            nc.gpsimd.memset(ones[:, :], 1.0).then_inc(ones_set, 1)
            nc.gpsimd.memset(NM[:, :, :], 0.0).then_inc(ones_set, 1)
            pool.wait_ge(ones_set, 2)
            for h in range(2):
                nc.gpsimd.memset(KC[OTHER[h], :, h, :].bitcast(f32), 0.0).then_inc(pads_set, 1)
                pool.wait_ge(pads_set, 3 * h + 1)
                nc.gpsimd.memset(QC[OTHER[h], :, h, :].bitcast(f32), 0.0).then_inc(pads_set, 1)
                pool.wait_ge(pads_set, 3 * h + 2)
                nc.gpsimd.memset(KC[AUX[h], :, h, :].bitcast(f32), 1.0).then_inc(pads_set, 1)
                pool.wait_ge(pads_set, 3 * h + 3)
            pool.wait_ge(wh_done, 1)
            nc.gpsimd.tensor_tensor(WL[:, :], W_raw, WH[:, :], ALU.subtract).then_inc(wl_done, 1)

            def normalise(n, s):
                t = 8 * n + s
                pool.wait_ge(rd_done, t + 1)
                pool.wait_ge(pv_evac, t + 1)
                if s % PAIRS == 0:
                    wait(pool, o_done, n)
                nc.gpsimd.tensor_tensor(AT[:, s % PAIRS, :], PVR[:, :], RD[:, :], ALU.mult).then_inc(norm_done, 1)

            def sum_blocks(n, s):
                t = 8 * n + s
                pool.wait_ge(exp_done, 4 * t + 4)
                wait(pool, den_done, t)
                e = probs[:, s % 2, :, :, :]
                nc.gpsimd.tensor_tensor(PSUMK[:, :, :], e[:, :, 0, :], e[:, :, 1, :], ALU.add).then_inc(sum_part, 1)
                pool.wait_ge(sum_part, 2 * t + 1)
                nc.gpsimd.tensor_tensor(PSUMK[:, :, :], PSUMK[:, :, :], e[:, :, 2, :], ALU.add).then_inc(sum_part, 1)
                pool.wait_ge(sum_part, 2 * t + 2)
                nc.gpsimd.tensor_tensor(PSUMK[:, :, :], PSUMK[:, :, :], e[:, :, 3, :], ALU.add).then_inc(sum_done, 1)

            def step(n, first, last):
                for s in range(PAIRS):
                    if not (first and s < 2):
                        normalise(n - int(s < 2), (s - 2) % PAIRS)
                    if not (first and s == 0):
                        sum_blocks(n - int(s < 1), (s - 1) % PAIRS)

            batches(pool, step)
            normalise(N - 1, 6)
            sum_blocks(N - 1, 7)
            normalise(N - 1, 7)

        @block.scalar
        def _(act):
            act.wait_ge(bias_tr, 1)
            nc.scalar.copy(bcol[:, 0:BIASES], misc[:, 0:BIASES]).then_inc(bias_col, 1)
            with act.Fori(0, N // 2) as m:
                for k in range(2):
                    n = 2 * m + k
                    act.wait_ge(bn_done, 4 * n + 4)
                    act.wait_ge(eps_set, 1)
                    nc.scalar.activation(std[:, k, :], mv[:, k, :, 1], ACT.Sqrt, bias=epst[:, :]).then_inc(std_done, 1)
                for k in range(2):
                    n = 2 * m + k
                    act.wait_ge(xt_done, n + 1)
                    nc.scalar.copy(XH[:, n, :], st[:, k, 0, :]).then_inc(xh_done, 1)
            for k in range(2):
                act.wait_ge(gw_tr, k + 1)
                nc.scalar.mul(gwH[:, 4 * k:4 * k + 4, :], mx[:, k, :].rearrange("p (w m) -> p w m", m=P),
                              0.5 if k else 1.0).then_inc(gw_hi, 1)
            act.wait_ge(ld_W, 16)
            nc.scalar.copy(WH[:, :], W_raw).then_inc(wh_done, 1)
            act.wait_ge(bias_half, 1)
            with act.Fori(0, N // 2) as m:
                for k in range(2):
                    n = 2 * m + k
                    act.wait_ge(state, n + 1)
                    nc.scalar.copy(DH, Dst).then_inc(state_hi, 1)
                    act.wait_ge(gates_done, 3 * n + 1)
                    nc.scalar.activation(tf, gate[k][0], ACT.Tanh, bias=bhalf[:, 0:1], scale=0.5).then_inc(t_done, 1)
                    act.wait_ge(gates_done, 3 * n + 2)
                    nc.scalar.activation(ti, gate[k][1], ACT.Tanh, bias=bhalf[:, 1:2], scale=0.5).then_inc(t_done, 1)
                    act.wait_ge(gates_done, 3 * n + 3)
                    nc.scalar.activation(tg, gate[k][2], ACT.Tanh, bias=bcol[:, B_C:B_C + 1]).then_inc(t_done, 1)
            act.wait_ge(state, N + 1)
            nc.scalar.copy(DH, Dst).then_inc(state_hi, 1)
            with act.Fori(0, N // 2) as m:
                for k in range(2):
                    n = 2 * m + k
                    act.wait_ge(h_done, n + 1)
                    nc.scalar.activation(HT[k], st[:, k, 0, :], ACT.Tanh, bias=bcol[:, B_O:B_O + 1]).then_inc(ht_done, 1)

            def evac_q(n, s):
                t = 8 * n + s
                act.wait_ge(q_done, t + 1)
                wait(act, q_lo, 2 * t - 2)
                nc.scalar.activation(Q32[:, s % 2, :], misc[:, :], ACT.Identity,
                                     bias=bcol[:, s % PAIRS:s % PAIRS + 1]).then_inc(q_evac, 1)

            def evac_k(n, s):
                t = 8 * n + s
                act.wait_ge(k_done, t + 1)
                wait(act, k_lo, 2 * t)
                nc.scalar.activation(K32[:, :], misc[:, :], ACT.Identity,
                                     bias=bcol[:, PAIRS + s % PAIRS:PAIRS + s % PAIRS + 1]).then_inc(k_evac, 1)

            def hi_q(n, s):
                t = 8 * n + s
                wait(act, st_done, 4 * t - 12)
                act.wait_ge(q_evac, t + 1)
                for h in range(2):
                    nc.scalar.copy(QB[OWN[h], s % 4, h, :], Q32[OWN[h], s % 2, :]).then_inc(q_hi, 1)

            def hi_k(n, s):
                t = 8 * n + s
                act.wait_ge(k_evac, t + 1)
                for h in range(2):
                    nc.scalar.copy(KA[OWN[h], s % 4, h, :], K32[OWN[h], :]).then_inc(k_hi, 1)

            def evac_v(group, half, tb, staged):
                act.wait_ge(v_done, group + 1)
                wait(act, d_vs[0], staged[0])
                wait(act, d_vs[1], staged[1])
                nc.scalar.copy(VALL[:, tb, half * L:(half + 1) * L], misc[:, :]).then_inc(v_evac, 1)

            def evac_pv(n, s):
                t = 8 * n + s
                act.wait_ge(pv_done, t + 1)
                wait(act, norm_done, t)
                nc.scalar.copy(PVR[:, :], pv[:, :]).then_inc(pv_evac, 1)

            def evac_o(n):
                act.wait_ge(o_done, n + 1)
                nc.scalar.activation(OT[:, :], misc[:, :], ACT.Identity, bias=bfin[:, :]).then_inc(o_evac, 1)

            def exps(n, s, u):
                t = 8 * n + s
                act.wait_ge(st_done, 4 * t + u + 1)
                wait(act, pv_done, t - 1)
                wait(act, sum_done, t - 1)
                kb = 2 * (u // 2)
                nc.scalar.activation(probs[:, s % 2, u % 2, kb:kb + 2, :], st[:, u % 2, :, :], ACT.Exp,
                                     scale=SCALE).then_inc(exp_done, 1)

            act.wait_ge(bias_fin, 1)
            act.wait_ge(out_rows, 16 * N)
            for tb in range(TB):
                evac_v(tb, 0, tb, (0, 0))
            for s in range(2):
                evac_q(0, s)
                evac_k(0, s)
                hi_q(0, s)
                hi_k(0, s)

            def step(n, first, last):
                for s in range(PAIRS):
                    ahead = not (last and s >= 6)
                    if s == 2 and not first:
                        evac_o(n - 1)
                    if ahead:
                        evac_q(n, s + 2)
                    exps(n, s, 0)
                    if ahead:
                        hi_q(n, s + 2)
                        evac_k(n, s + 2)
                    exps(n, s, 1)
                    if ahead:
                        hi_k(n, s + 2)
                    if s < 4:
                        evac_v(4 + 8 * n + s, 1, s, (64 * n, 64 * n))
                    elif not last:
                        evac_v(4 + 8 * n + s, 0, s - 4, (64 * n + 32, 64 * n + 32))
                    exps(n, s, 2)
                    if not (first and s == 0):
                        evac_pv(n, s - 1)
                    exps(n, s, 3)

            batches(act, step)
            evac_pv(N - 1, 7)
            evac_o(N - 1)

        @block.vector
        def _(dve):
            nc.vector.memset(epst[:, :], EPS).then_inc(eps_set, 1)
            with dve.Fori(0, N // 2) as m:
                for k in range(2):
                    n = 2 * m + k
                    if k == 0:
                        dve.wait_ge(ld_x, 16 * m + 16)
                    for b in range(TB):
                        nc.vector.bn_stats(stats[:, TB * k + b, :], x_all[:, n, b, :]).then_inc(bn_part, 1)
                    for b in range(TB):
                        dve.wait_ge(bn_part, 4 * n + b + 1)
                        dve.sem_inc(passed_dve, 1)
                        nc.vector.bn_aggr(mv[:, k, b, :], stats[:, TB * k + b, :]).then_inc(bn_done, 1)
                for k in range(2):
                    n = 2 * m + k
                    dve.wait_ge(std_done, n + 1)
                    nc.vector.reciprocal(rstd[:, k, :], std[:, k, :]).then_inc(rstd_done, 1)
                    dve.wait_ge(rstd_done, n + 1)
                    for b in range(TB):
                        nc.vector.tensor_scalar(xn[:, k, b, :], x_all[:, n, b, :], mv[:, k, b, 0:1],
                                                rstd[:, k, b:b + 1], ALU.subtract, ALU.mult).then_inc(xn_done, 1)
                for k in range(2):
                    n = 2 * m + k
                    dve.wait_ge(xh_done, n + 1)
                    nc.vector.tensor_tensor(XL[:, n, :], st[:, k, 0, :], XH[:, n, :], ALU.subtract).then_inc(xl_done, 1)
            for k in range(2):
                dve.wait_ge(gw_hi, k + 1)
                nc.vector.scalar_tensor_tensor(gwL[:, 4 * k:4 * k + 4, :],
                                               mx[:, k, :].rearrange("p (w m) -> p w m", m=P), 0.5 if k else 1.0,
                                               gwH[:, 4 * k:4 * k + 4, :], ALU.mult, ALU.subtract).then_inc(gw_lo, 1)
            dve.wait_ge(bias_col, 1)
            nc.vector.tensor_scalar(bhalf[:, :], bcol[:, B_F:B_F + 2], 0.5, None, ALU.mult).then_inc(bias_half, 1)
            dve.wait_ge(bias_fold, 1)
            nc.vector.tensor_tensor(bfin[:, :], misc[:, 0:1], bcol[:, B_OUT:B_OUT + 1], ALU.add).then_inc(bias_fin, 1)
            nc.vector.tensor_scalar(Dst, bcol[:, IN_C:IN_C + 1].to_broadcast([P, L]), 2.0, None,
                                    ALU.mult).then_inc(state, 1)
            with dve.Fori(0, N) as n:
                dve.wait_ge(state_hi, n + 1)
                nc.vector.tensor_tensor(DL, Dst, DH, ALU.subtract).then_inc(state_lo, 1)
                dve.wait_ge(t_done, 3 * n + 1)
                nc.vector.scalar_tensor_tensor(Abuf, tf, 1.0, Dst, ALU.add, ALU.mult).then_inc(ab_done, 1)
                dve.wait_ge(t_done, 3 * n + 3)
                nc.vector.scalar_tensor_tensor(Bbuf, ti, 1.0, tg, ALU.add, ALU.mult).then_inc(ab_done, 1)
                dve.wait_ge(ab_done, 2 * n + 2)
                nc.vector.scalar_tensor_tensor(Dst, Abuf, 0.5, Bbuf, ALU.mult, ALU.add).then_inc(state, 1)
            dve.wait_ge(state_hi, N + 1)
            nc.vector.tensor_tensor(DL, Dst, DH, ALU.subtract).then_inc(state_lo, 1)
            with dve.Fori(0, N // 2) as m:
                for k in range(2):
                    n = 2 * m + k
                    dve.wait_ge(htr_done, n + 1)
                    nc.vector.tensor_tensor(rsum[:, n, :, :],
                                            st[:, k, 1, :].rearrange("p (b d) -> p b d", d=D), x_all[:, n, :, :],
                                            ALU.add).then_inc(r_done, 1)

            def lo_k(n, s):
                t = 8 * n + s
                for h in range(2):
                    dve.wait_ge(k_hi, 2 * t + h + 1)
                    nc.vector.tensor_tensor(KA[OTHER[h], s % 4, h, :], K32[OWN[h], :], KA[OWN[h], s % 4, h, :],
                                            ALU.subtract).then_inc(k_lo, 1)

            def lo_q(n, s):
                t = 8 * n + s
                wait(dve, st_done, 4 * t - 4)
                for h in range(2):
                    dve.wait_ge(q_hi, 2 * t + h + 1)
                    nc.vector.tensor_tensor(QC[OWN[h], s % 2, h, :], Q32[OWN[h], s % 2, :], QB[OWN[h], s % 4, h, :],
                                            ALU.subtract).then_inc(q_lo, 1)

            def maxima(n, s, js):
                t = 8 * n + s
                for j in js:
                    if j == 0:
                        wait(dve, tm_done, t)
                    dve.wait_ge(mx_done, 8 * t + j + 1)
                    nc.vector.tensor_reduce(NM[:, j // 4, j % 4:j % 4 + 1], mx[:, j % 2, :], AX.X, ALU.max,
                                            negate=True).then_inc(red_done, 1)

            def turn_max(n, s):
                t = 8 * n + s
                dve.wait_ge(red_done, 8 * t + 8)
                wait(dve, d_m[s % 2], 128 * (4 * n + s // 2))
                nc.vector.transpose(TM[:, s % 2, :], NM[:, :, :].rearrange("p h c -> p (h c)")).then_inc(tm_done, 1)

            def divisors(n, s):
                t = 8 * n + s
                dve.wait_ge(den_done, t + 1)
                wait(dve, rd_done, t)
                nc.vector.transpose(DT[:, :], misc[:, :]).then_inc(den_used, 1)
                dve.wait_ge(den_used, t + 1)
                nc.vector.reciprocal(R16[:, :], DT[:, :].rearrange("p (c j) -> p c j", j=32)[:, :, 0]).then_inc(r16_done, 1)
                dve.wait_ge(r16_done, t + 1)
                wait(dve, norm_done, t)
                nc.vector.transpose(RD[:, :].rearrange("p (c j) -> p c j", j=32),
                                    R16[:, :].unsqueeze(2).to_broadcast([P, L // 32, 32])).then_inc(rd_done, 1)

            def finish(n):
                dve.wait_ge(tr_done, n + 1)
                dve.wait_ge(d_res, 16 * n + 16)
                dve.wait_ge(out_rows, 16 * (N + n))
                nc.vector.tensor_tensor(OUTB[:, :, :], misc[:, :].rearrange("p (b d) -> p b d", d=D), RES[:, :, :],
                                        ALU.add).then_inc(out_done, 1)

            dve.wait_ge(out_rows, 16 * N)
            dve.wait_ge(ones_set, 2)
            lo_k(0, 0)
            lo_k(0, 1)
            lo_q(0, 0)
            maxima(0, 0, range(8))
            turn_max(0, 0)

            def step(n, first, last):
                for s in range(PAIRS):
                    if not (last and s == 7):
                        lo_q(n, s + 1)
                        maxima(n, s + 1, range(0, 6))
                        maxima(n, s + 1, range(6, 8))
                        turn_max(n, s + 1)
                    if not (last and s >= 6):
                        lo_k(n, s + 2)
                    if not (first and s == 0):
                        divisors(n, s - 1)
                    if s == 2 and not first:
                        finish(n - 1)

            batches(dve, step)
            divisors(N - 1, 7)
            finish(N - 1)

        @block.tensor
        def _(pe):
            def product(dst, terms):
                for i, (stationary, moving) in enumerate(terms):
                    last = nc.tensor.matmul(dst, stationary, moving, start=(i == 0), stop=(i == len(terms) - 1))
                return last

            pe.wait_ge(id1, 1)
            pe.wait_ge(ld_b, 16 * 7)
            nc.tensor.transpose(misc[:, 0:BIASES], brow[0:BIASES, :], ident[0:BIASES, 0:BIASES]).then_inc(bias_tr, 1)
            with pe.Fori(0, N // 2) as m:
                for k in range(2):
                    n = 2 * m + k
                    pe.wait_ge(xn_done, 4 * n + 4)
                    for b in range(TB):
                        last = nc.tensor.transpose(st[:, k, 0, b * P:(b + 1) * P], xn[:, k, b, :], ident[:, :])
                    last.then_inc(xt_done, 1)
            pe.wait_ge(ld_w, 16 * 8)
            for k in range(2):
                for i in range(4):
                    last = nc.tensor.transpose(mx[:, k, i * P:(i + 1) * P], w_raw[:, 4 * k + i, :], ident[:, :])
                last.then_inc(gw_tr, 1)
            pe.wait_ge(ld_wo, 16)
            pe.wait_ge(bias_col, 1)
            for c in range(PAIRS):
                last = nc.tensor.matmul(misc[:, 0:1], WO[:, c, :], bcol[:, B_V + c:B_V + c + 1], start=(c == 0),
                                        stop=(c == PAIRS - 1))
            last.then_inc(bias_fold, 1)
            pe.wait_ge(gw_lo, 2)
            pe.wait_ge(xl_done, N)
            with pe.Fori(0, N // 2) as m:
                for k in range(2):
                    n = 2 * m + k
                    for g in range(3):
                        for i, (w, x) in enumerate(((gwH, XH), (gwL, XH), (gwH, XL))):
                            nc.tensor.matmul(gate[k][g], w[:, g, :], x[:, n, :], start=(i == 0), stop=False)
                    pe.wait_ge(state_hi, n + 1)
                    for g in range(3):
                        nc.tensor.matmul(gate[k][g], gwH[:, 4 + g, :], DH, start=False, stop=False)
                        nc.tensor.matmul(gate[k][g], gwL[:, 4 + g, :], DH, start=False, stop=False)
                    pe.wait_ge(state_lo, n + 1)
                    for g in range(3):
                        nc.tensor.matmul(gate[k][g], gwH[:, 4 + g, :], DL, start=False,
                                         stop=True).then_inc(gates_done, 1)
            pe.wait_ge(state_lo, N + 1)
            with pe.Fori(0, N // 2) as m:
                for k in range(2):
                    n = 2 * m + k
                    product(st[:, k, 0, :], [(gwH[:, 3, :], XH[:, n, :]), (gwL[:, 3, :], XH[:, n, :]),
                                             (gwH[:, 3, :], XL[:, n, :]), (gwH[:, 7, :], DH), (gwL[:, 7, :], DH),
                                             (gwH[:, 7, :], DL)]).then_inc(h_done, 1)
                for k in range(2):
                    n = 2 * m + k
                    pe.wait_ge(ht_done, n + 1)
                    for b in range(TB):
                        last = nc.tensor.transpose(st[:, k, 1, b * P:(b + 1) * P], HT[k][:, b * P:(b + 1) * P],
                                                   ident[:, :])
                    last.then_inc(htr_done, 1)
                pe.wait_ge(r_done, 2 * m + 2)

            def project(n, s, column, done):
                nn = n + s // PAIRS
                c = slice(column + (s % PAIRS) * P, column + (s % PAIRS) * P + P)
                product(misc[:, :], [(WH[:, c], XH[:, nn, :]), (WL[:, c], XH[:, nn, :]),
                                     (WH[:, c], XL[:, nn, :])]).then_inc(done, 1)

            def project_v(half, tb):
                c = slice(2 * DIM + half * L, 2 * DIM + (half + 1) * L)
                b = slice(tb * P, (tb + 1) * P)
                product(misc[:, :], [(XSH[:, b], WH[:, c]), (XSL[:, b], WH[:, c]),
                                     (XSH[:, b], WL[:, c])]).then_inc(v_done, 1)

            def scores_for_max(n, s, js):
                t = 8 * n + s
                for j in js:
                    h, b = j // 4, j % 4
                    if j == 0:
                        pe.wait_ge(d_dup[s % 2], dmas(n, s, 2))
                        pe.wait_ge(k_lo, 2 * t + 2)
                    wait(pe, red_done, 8 * t + j - 1)
                    nc.tensor.matmul(mx[:, j % 2, :], QB[:, s % 4, h, b * P:(b + 1) * P], KA[:, s % 4, h, :],
                                     start=True, stop=True).then_inc(mx_done, 1)

            def scores(n, s, u):
                t = 8 * n + s
                h = u % 2
                if u == 0:
                    pe.wait_ge(d_kc[s % 2], dmas(n, s, 2))
                    pe.wait_ge(d_m[s % 2], dmas(n, s, 8))
                    pe.wait_ge(q_lo, 2 * t + 2)
                wait(pe, exp_done, 4 * t + u - 1)
                for i in range(2):
                    kb = 2 * (u // 2) + i
                    b = slice(kb * P, (kb + 1) * P)
                    nc.tensor.matmul(st[:, h, i, :], KA[:, s % 4, h, b], QB[:, s % 4, h, :], start=True, stop=False)
                    last = nc.tensor.matmul(st[:, h, i, :], KC[:, s % 2, h, b], QC[:, s % 2, h, :], start=False,
                                            stop=True)
                last.then_inc(st_done, 1)

            def values(n, s, kb):
                t = 8 * n + s
                if kb == 0:
                    pe.wait_ge(exp_done, 4 * t + 4)
                    pe.wait_ge(d_vs[s % 2], dmas(n, s, 1))
                    wait(pe, pv_evac, t)
                for h in range(2):
                    last = nc.tensor.matmul(pv[OWN[h], :], VS[:, s % 2, kb, h * HD:(h + 1) * HD],
                                            probs[:, s % 2, h, kb, :], start=(kb == 0), stop=(kb == TB - 1))
                if kb == TB - 1:
                    last.then_inc(pv_done, 1)

            def sums(n, s):
                t = 8 * n + s
                pe.wait_ge(sum_done, t + 1)
                for h in range(2):
                    last = nc.tensor.matmul(misc[OWN[h], :], ones[:, :], PSUMK[:, h, :], start=True, stop=True)
                last.then_inc(den_done, 1)

            def project_out():
                product(misc[:, :], [(WO[:, c, :], AT[:, c, :]) for c in range(PAIRS)]).then_inc(o_done, 1)

            def turn_out(n):
                pe.wait_ge(o_evac, n + 1)
                for b in range(TB):
                    last = nc.tensor.transpose(misc[:, b * P:(b + 1) * P], OT[:, b * P:(b + 1) * P], ident[:, :])
                last.then_inc(tr_done, 1)

            pe.wait_ge(out_rows, 16 * N)
            pe.wait_ge(bias_fin, 1)
            pe.wait_ge(wl_done, 1)
            pe.wait_ge(d_xs, 32)
            for tb in range(TB):
                wait(pe, v_evac, tb)
                project_v(0, tb)
            pe.wait_ge(v_evac, TB)
            for s in range(2):
                wait(pe, k_evac, s)
                project(0, s, 0, q_done)
                pe.wait_ge(q_evac, s + 1)
                project(0, s, DIM, k_done)
            scores_for_max(0, 0, range(8))
            pe.wait_ge(ones_set, 1)
            pe.wait_ge(pads_set, 6)

            def step(n, first, last):
                for s in range(PAIRS):
                    t = 8 * n + s
                    ahead = not (last and s >= 6)
                    if not (last and s == 7):
                        scores_for_max(n, s + 1, range(0, 3))
                    if s == 2 and not first:
                        pe.wait_ge(o_evac, n)
                    elif s == 3 and not first:
                        pe.wait_ge(out_done, n)
                    elif first and s <= 1:
                        pe.wait_ge(v_evac if s else k_evac, 5 if s else 2)
                    else:
                        pe.wait_ge(den_used, t - 1)
                    if ahead:
                        project(n, s + 2, 0, q_done)
                    if not (first and s == 0):
                        values(n, s - 1, 0)
                    scores(n, s, 0)

                    if not (last and s == 7):
                        scores_for_max(n, s + 1, range(3, 6))
                    if ahead:
                        pe.wait_ge(q_evac, t + 3)
                        project(n, s + 2, DIM, k_done)
                    if not (first and s == 0):
                        values(n, s - 1, 1)
                    scores(n, s, 1)

                    if not (last and s == 7):
                        scores_for_max(n, s + 1, range(6, 8))
                    if ahead:
                        pe.wait_ge(k_evac, t + 3)
                    if s == 4 and not last:
                        pe.wait_ge(d_xs, 32 * n + 64)
                    if s < 4:
                        project_v(1, s)
                    elif not last:
                        project_v(0, s - 4)
                    if not (first and s == 0):
                        values(n, s - 1, 2)
                    scores(n, s, 2)

                    if s < 4 or not last:
                        pe.wait_ge(v_evac, 4 + t + 1)
                    if not (first and s == 0):
                        sums(n, s - 1)
                        values(n, s - 1, 3)
                    scores(n, s, 3)
                    if s == 1 and not first:
                        pe.wait_ge(den_used, t)
                        pe.wait_ge(norm_done, 8 * n)
                        project_out()
                    if s == 2 and not first:
                        pe.wait_ge(den_used, t)
                        turn_out(n - 1)

            batches(pe, step)
            for kb in range(TB):
                values(N - 1, 7, kb)
            pe.wait_ge(den_used, 8 * N - 1)
            sums(N - 1, 7)
            pe.wait_ge(den_used, 8 * N)
            pe.wait_ge(norm_done, 8 * N)
            project_out()
            turn_out(N - 1)


_INS = ['L0_attn_data', 'L0_attn_W_qkv', 'L0_attn_b_qkv', 'L0_attn_W_out', 'L0_attn_b_out', 'L0_ffn_wf', 'L0_ffn_uf',
        'L0_ffn_bf', 'L0_ffn_wi', 'L0_ffn_ui', 'L0_ffn_bi', 'L0_ffn_wc', 'L0_ffn_uc', 'L0_ffn_bc', 'L0_ffn_wo',
        'L0_ffn_uo', 'L0_ffn_bo', 'L0_ffn_in_c']


def kernel(**inputs):
    import numpy as _np
    import concourse.bacc as _bacc
    from concourse import mybir as _mybir
    from concourse.bass_utils import run_bass_kernel_spmd as _run

    nc = _bacc.Bacc("TRN2", target_bir_lowering=False, num_devices=1)
    arrays, args = {}, []
    for name in _INS:
        a = _np.ascontiguousarray(inputs[name])
        arrays[f"in_{name}_dram"] = a
        args.append(nc.dram_tensor(f"in_{name}_dram", a.shape, _mybir.dt.from_np(a.dtype), kind="ExternalInput").ap())
    shape = arrays["in_L0_attn_data_dram"].shape
    args.append(nc.dram_tensor("out_dram", shape, _mybir.dt.float32, kind="ExternalOutput").ap())
    build_block(nc, *args)
    r = _run(nc, [arrays], core_ids=[0])
    return r.results[0]["out_dram"]
```

```python
import concourse.bass as bass
from concourse import mybir
from contextlib import ExitStack


def build_block(nc, data, W_qkv, b_qkv, W_out, b_out, wf, uf, bf, wi, ui, bi, wc, uc, bc, wo, uo, bo, in_c, out):
    f32 = mybir.dt.float32
    f32r = mybir.dt.float32r
    ALU = mybir.AluOpType
    ACT = mybir.ActivationFunctionType
    AX = mybir.AxisListType

    P = 128
    N, L, D = data.shape
    DIM = W_qkv.shape[1] // 3
    PAIRS = DIM // P
    HD = P // 2
    TB = L // P
    SCALE = float(HD) ** -0.5
    EPS = 1e-5
    HALVES = 2
    BIASES = 3 * PAIRS + 6
    B_V, B_OUT, B_F, B_I, B_C, B_O, IN_C = 2 * PAIRS, 3 * PAIRS, 25, 26, 27, 28, 29
    OWN = [slice(0, HD), slice(HD, P)]
    OTHER = [slice(HD, P), slice(0, HD)]
    AUX = [slice(HD, HD + 1), slice(0, 1)]

    data_t = data.rearrange("n (b p) d -> p n b d", p=P)
    out_t = out.rearrange("n (b p) d -> p n b d", p=P)
    Wo_v = W_out.rearrange("(c p) d -> p c d", p=P)

    ctx = ExitStack()
    with ctx:
        def sb(name, shape, dt=f32):
            return ctx.enter_context(nc.sbuf_tensor(name, shape, dt))

        def sem(name):
            return ctx.enter_context(nc.semaphore(name))

        ident = sb("ident", [P, P])
        ones = sb("ones", [P, HD])
        bcol = sb("bcol", [P, 32])
        bhalf = sb("bhalf", [P, 2])
        bfin = sb("bfin", [P, 1])
        probs = sb("probs", [P, 2, 2, TB, L])
        XH = sb("XH", [P, N, L], f32r)
        XL = sb("XL", [P, N, L], f32r)
        WH = sb("WH", [P, 3 * DIM], f32r)
        WL = sb("WL", [P, 3 * DIM], f32r)
        WO = sb("WO", [P, PAIRS, D])
        VALL = sb("VALL", [P, TB, DIM])
        XSH = sb("XSH", [P, L], f32r)
        XSL = sb("XSL", [P, L], f32r)
        VS = sb("VS", [P, 2, TB, P])
        Q32 = sb("Q32", [P, 2, L])
        QB = sb("QB", [P, 4, 2, L], f32r)
        KA = sb("KA", [P, 4, 2, L], f32r)
        QC = sb("QC", [P, 2, 2, L], f32r)
        KC = sb("KC", [P, 2, 2, L], f32r)
        PSUMK = sb("PSUMK", [P, 2, L])
        R16 = sb("R16", [P, L // 32])
        RD = sb("RD", [P, L])
        AT = sb("AT", [P, PAIRS, L])
        OT = sb("OT", [P, L])
        RES = sb("RES", [P, TB, D])
        gwH = sb("gwH", [P, 8, P], f32r)
        gwL = sb("gwL", [P, 8, P], f32r)
        DH = sb("DH", [P, L], f32r)
        DL = sb("DL", [P, L], f32r)
        NM = sb("NM", [P, 2 * TB])
        TM = sb("TM", [2 * TB, P])
        epst = sb("epst", [P, 1])

        x_all = probs[:, 0, :, :, :].rearrange("p a b l -> p (a b l)").rearrange("p (n b d) -> p n b d", n=N, d=D)
        rest = probs[:, 1, :, :, :].rearrange("p a b l -> p (a b l)")
        W_raw = rest[:, 0:3 * DIM]
        w_raw = rest[:, 3 * DIM:3 * DIM + 8 * P].rearrange("p (w i) -> p w i", w=8)
        xn = AT[:, 0:2, :].rearrange("p a (b d) -> p a b d", d=D)
        brow = AT[0:32, 2, 0:P]
        stats = AT[:, 3, 0:12 * TB].rearrange("p (b c) -> p b c", c=6)
        mv = AT[:, 3, P:P + 4 * TB].rearrange("p (k b c) -> p k b c", k=2, c=2)
        std = AT[:, 3, 2 * P:2 * P + 2 * TB].rearrange("p (k b) -> p k b", k=2)
        rstd = AT[:, 3, 3 * P:3 * P + 2 * TB].rearrange("p (k b) -> p k b", k=2)
        state, tf, ti, tg = OT[:, :], RES[:, :, :].rearrange("p b d -> p (b d)"), AT[:, 7, :], AT[:, 6, :]

        st = ctx.enter_context(nc.psum_tensor("st", [P, 2, 2, L], f32))
        mx = ctx.enter_context(nc.psum_tensor("mx", [P, 2, L], f32))
        pv = ctx.enter_context(nc.psum_tensor("pv", [P, L], f32))
        misc = ctx.enter_context(nc.psum_tensor("misc", [P, L], f32))

        passed_sp, passed_dve = sem("passed_sp"), sem("passed_dve")
        ld_x0 = sem("ld_x0")
        ld_b, ld_x, ld_w, ld_W, ld_wo = sem("ld_b"), sem("ld_x"), sem("ld_w"), sem("ld_W"), sem("ld_wo")
        id0, id1, ones_set, pads_set, eps_set = sem("id0"), sem("id1"), sem("ones_set"), sem("pads_set"), sem("eps_set")
        bias_tr, bias_col, bias_half, bias_fold, bias_fin = (sem("bias_tr"), sem("bias_col"), sem("bias_half"),
                                                             sem("bias_fold"), sem("bias_fin"))
        gw_tr, gw_hi, gw_lo = sem("gw_tr"), sem("gw_hi"), sem("gw_lo")
        bn_part, bn_done, std_done, rstd_done, xn_done, xt_done, xh_done, xl_done = (
            sem("bn_part"), sem("bn_done"), sem("std_done"), sem("rstd_done"), sem("xn_done"), sem("xt_done"),
            sem("xh_done"), sem("xl_done"))
        wh_done, wl_done = sem("wh_done"), sem("wl_done")
        state_done, state_hi, state_lo, gate_done, t_done, ab_done, h_done, ht_done = (
            sem("state_done"), sem("state_hi"), sem("state_lo"), sem("gate_done"), sem("t_done"), sem("ab_done"),
            sem("h_done"), sem("ht_done"))
        q_done, k_done, v_done, den_done, o_done, tr_done = (
            sem("q_done"), sem("k_done"), sem("v_done"), sem("den_done"), sem("o_done"), sem("tr_done"))
        st_done, mx_done, pv_done = sem("st_done"), sem("mx_done"), sem("pv_done")
        q_evac, v_evac, q_hi, k_hi, exp_done, pv_evac, o_evac = (
            sem("q_evac"), sem("v_evac"), sem("q_hi"), sem("k_hi"), sem("exp_done"),
            sem("pv_evac"), sem("o_evac"))
        q_lo, k_lo, red_done, max_turned, tm_done, den_used, r16_done, rd_done, out_done = (
            sem("q_lo"), sem("k_lo"), sem("red_done"), sem("max_turned"), sem("tm_done"), sem("den_used"), sem("r16_done"),
            sem("rd_done"), sem("out_done"))
        sum_part, sum_done, norm_done = sem("sum_part"), sem("sum_done"), sem("norm_done")
        d_dup = [sem("d_dup0"), sem("d_dup1")]
        d_kc = [sem("d_kc0"), sem("d_kc1")]
        d_m = [sem("d_m0"), sem("d_m1")]
        d_vs = [sem("d_vs0"), sem("d_vs1")]
        d_xs, d_res, out_rows = sem("d_xs"), sem("d_res"), sem("out_rows")

        def wait(eng, s, value):
            if not (isinstance(value, int) and value <= 0):
                eng.wait_ge(s, value)

        def dmas(n, s, each):
            return (4 * n + s // 2 + 1) * (16 * each)

        def batches(eng, step):
            step(0, True, False)
            with eng.Fori(1, N - 1) as n:
                step(n, False, False)
            step(N - 1, False, True)

        block = ctx.enter_context(nc.Block())

        @block.sync
        def _(sp):
            sp.dma_start(x_all[:, 0:2, :, :], data_t[:, 0:2, :, :]).then_inc(ld_x0, 16)
            sp.dma_start(brow[0:3 * PAIRS, :], b_qkv.rearrange("(c r) -> c r", r=P)).then_inc(ld_b, 16)
            for i, v in enumerate((b_out, bf, bi, bc, bo, in_c)):
                sp.dma_start(brow[B_OUT + i:B_OUT + i + 1, :], v.rearrange("(a r) -> a r", a=1)).then_inc(ld_b, 16)
            for n in range(2, N, 2):
                sp.dma_start(x_all[:, n:n + 2, :, :], data_t[:, n:n + 2, :, :]).then_inc(ld_x, 16)
            sp.dma_start(W_raw, W_qkv).then_inc(ld_W, 16)
            for i, w in enumerate((wf, wi, wc, wo, uf, ui, uc, uo)):
                sp.dma_start(w_raw[:, i, :], w).then_inc(ld_w, 16)
            sp.dma_start(WO[:, :, :], Wo_v).then_inc(ld_wo, 16)

            def stage_x(n):
                sp.wait_ge(xl_done, N)
                sp.dma_start(XSH[:, :].bitcast(f32), XH[:, n, :].bitcast(f32)).then_inc(d_xs, 16)
                sp.dma_start(XSL[:, :].bitcast(f32), XL[:, n, :].bitcast(f32)).then_inc(d_xs, 16)

            def duplicate_q(n, s):
                t = 8 * n + s
                sp.wait_ge(q_hi, 2 * t + 2)
                sp.sem_inc(passed_sp, 1)
                for h in range(2):
                    sp.dma_start(QB[OTHER[h], s % 4, h, :].bitcast(f32), QB[OWN[h], s % 4, h, :].bitcast(f32)).then_inc(d_dup[s % 2], 16)

            def copy_k(n, s):
                t = 8 * n + s
                wait(sp, st_done, 4 * t - 4)
                sp.sem_inc(passed_sp, 1)
                sp.wait_ge(k_hi, 2 * t + 2)
                sp.sem_inc(passed_sp, 1)
                for h in range(2):
                    sp.dma_start(KC[OWN[h], s % 2, h, :].bitcast(f32), KA[OWN[h], s % 4, h, :].bitcast(f32)).then_inc(d_kc[s % 2], 16)

            def place_max(n, s):
                t = 8 * n + s
                sp.wait_ge(tm_done, t + 1)
                sp.sem_inc(passed_sp, 1)
                for h in range(2):
                    sp.dma_start(QC[AUX[h], s % 2, h, :].bitcast(f32).rearrange("p (b j) -> p b j", j=P),
                                 TM[TB * h:TB * h + TB, :]).then_inc(d_m[s % 2], 16)

            stage_x(0)
            sp.wait_ge(pads_set, 6)
            duplicate_q(0, 0)
            copy_k(0, 0)
            duplicate_q(0, 1)
            place_max(0, 0)

            def step(n, first, last):
                for s in range(PAIRS):
                    t = 8 * n + s
                    if not (last and s == 7):
                        copy_k(n, s + 1)
                    sp.wait_ge(v_evac, 8 * n + (4 if s < 4 else 8))
                    sp.sem_inc(passed_sp, 1)
                    wait(sp, pv_done, t - 1)
                    sp.sem_inc(passed_sp, 1)
                    sp.dma_start(VS[:, s % 2, :, :], VALL[:, :, s * P:(s + 1) * P]).then_inc(d_vs[s % 2], 16)
                    if s == 0 and not first:
                        sp.wait_ge(state_lo, N + 1)
                        sp.dma_start(RES[:, :, :], data_t[:, n - 1, :, :]).then_inc(d_res, 16)
                    if s == 3 and not first:
                        sp.wait_ge(out_done, n)
                        sp.sem_inc(passed_sp, 1)
                        sp.dma_start(out_t[:, n - 1, :, :], RES[:, :, :]).then_inc(out_rows, 16)
                    if s == 7 and not first:
                        sp.wait_ge(out_rows, 16 * n)
                        sp.sem_inc(passed_sp, 1)
                    if s == 4 and not last:
                        sp.wait_ge(v_done, 8 * n + 8)
                        sp.sem_inc(passed_sp, 1)
                        stage_x(n + 1)
                    if not (last and s >= 6):
                        duplicate_q(n, s + 2)
                    if not (last and s == 7):
                        place_max(n, s + 1)

            batches(sp, step)
            sp.dma_start(RES[:, :, :], data_t[:, N - 1, :, :]).then_inc(d_res, 16)
            sp.wait_ge(out_done, N)
            sp.dma_start(out_t[:, N - 1, :, :], RES[:, :, :]).then_inc(out_rows, 16)
            sp.wait_ge(out_rows, 16 * N)

        @block.gpsimd
        def _(pool):
            nc.gpsimd.memset(ident[:, :], 0.0).then_inc(id0, 1)
            pool.wait_ge(id0, 1)
            nc.gpsimd.affine_select(out=ident[:, :], in_=ident[:, :], compare_op=ALU.not_equal, fill=1.0, base=0,
                                    pattern=[[-1, P]], channel_multiplier=1).then_inc(id1, 1)
            nc.gpsimd.memset(ones[:, :], 1.0).then_inc(ones_set, 1)
            pool.wait_ge(ones_set, 1)
            for h in range(2):
                nc.gpsimd.memset(KC[OTHER[h], :, h, :].bitcast(f32), 0.0).then_inc(pads_set, 1)
                pool.wait_ge(pads_set, 3 * h + 1)
                nc.gpsimd.memset(QC[OTHER[h], :, h, :].bitcast(f32), 0.0).then_inc(pads_set, 1)
                pool.wait_ge(pads_set, 3 * h + 2)
                nc.gpsimd.memset(KC[AUX[h], :, h, :].bitcast(f32), 1.0).then_inc(pads_set, 1)
                pool.wait_ge(pads_set, 3 * h + 3)
            pool.wait_ge(wh_done, 1)
            nc.gpsimd.tensor_tensor(WL[:, :], W_raw, WH[:, :], ALU.subtract).then_inc(wl_done, 1)

            def normalise(n, s):
                t = 8 * n + s
                pool.wait_ge(rd_done, t + 1)
                pool.wait_ge(pv_evac, t + 1)
                nc.gpsimd.tensor_tensor(AT[:, s % PAIRS, :], AT[:, s % PAIRS, :], RD[:, :], ALU.mult).then_inc(norm_done, 1)

            def sum_blocks(n, s):
                t = 8 * n + s
                pool.wait_ge(exp_done, 4 * t + 4)
                wait(pool, den_done, t)
                e = probs[:, s % 2, :, :, :]
                nc.gpsimd.tensor_tensor(PSUMK[:, :, :], e[:, :, 0, :], e[:, :, 1, :], ALU.add).then_inc(sum_part, 1)
                pool.wait_ge(sum_part, 2 * t + 1)
                nc.gpsimd.tensor_tensor(PSUMK[:, :, :], PSUMK[:, :, :], e[:, :, 2, :], ALU.add).then_inc(sum_part, 1)
                pool.wait_ge(sum_part, 2 * t + 2)
                nc.gpsimd.tensor_tensor(PSUMK[:, :, :], PSUMK[:, :, :], e[:, :, 3, :], ALU.add).then_inc(sum_done, 1)

            def step(n, first, last):
                for s in range(PAIRS):
                    if not (first and s < 2):
                        normalise(n - int(s < 2), (s - 2) % PAIRS)
                    if not (first and s == 0):
                        sum_blocks(n - int(s < 1), (s - 1) % PAIRS)

            batches(pool, step)
            normalise(N - 1, 6)
            sum_blocks(N - 1, 7)
            normalise(N - 1, 7)

        @block.scalar
        def _(act):
            act.wait_ge(bias_tr, 1)
            nc.scalar.copy(bcol[:, 0:BIASES], misc[:, 0:BIASES]).then_inc(bias_col, 1)
            with act.Fori(0, N // 2) as m:
                for k in range(2):
                    n = 2 * m + k
                    act.wait_ge(bn_done, 4 * n + 4)
                    act.wait_ge(eps_set, 1)
                    nc.scalar.activation(std[:, k, :], mv[:, k, :, 1], ACT.Sqrt, bias=epst[:, :]).then_inc(std_done, 1)
                for k in range(2):
                    n = 2 * m + k
                    act.wait_ge(xt_done, n + 1)
                    nc.scalar.copy(XH[:, n, :], st[:, k, 0, :]).then_inc(xh_done, 1)
            for k in range(2):
                act.wait_ge(gw_tr, k + 1)
                nc.scalar.mul(gwH[:, 4 * k:4 * k + 4, :], mx[:, k, :].rearrange("p (w m) -> p w m", m=P),
                              0.5 if k else 1.0).then_inc(gw_hi, 1)
            act.wait_ge(ld_W, 16)
            nc.scalar.copy(WH[:, :], W_raw).then_inc(wh_done, 1)

            def tanh_gate(s, g):
                act.wait_ge(gate_done, 3 * s + g + 1)
                nc.scalar.activation((tf, ti, tg)[g], misc[:, :], ACT.Tanh,
                                     bias=bcol[:, B_C:B_C + 1] if g == 2 else bhalf[:, g:g + 1],
                                     scale=1.0 if g == 2 else 0.5).then_inc(t_done, 1)

            def hi_state(step):
                act.wait_ge(state_done, step + 1)
                nc.scalar.copy(DH[:, :], state).then_inc(state_hi, 1)

            def tanh_h(n):
                act.wait_ge(h_done, n + 1)
                nc.scalar.activation(OT[:, :], misc[:, :], ACT.Tanh, bias=bcol[:, B_O:B_O + 1]).then_inc(ht_done, 1)

            def evac_q(n, s):
                t = 8 * n + s
                act.wait_ge(q_done, t + 1)
                wait(act, q_lo, 2 * t - 2)
                nc.scalar.activation(Q32[:, s % 2, :], misc[:, :], ACT.Identity,
                                     bias=bcol[:, s % PAIRS:s % PAIRS + 1]).then_inc(q_evac, 1)

            def hi_q(n, s):
                t = 8 * n + s
                wait(act, st_done, 4 * t - 12)
                act.wait_ge(q_evac, t + 1)
                for h in range(2):
                    nc.scalar.copy(QB[OWN[h], s % 4, h, :], Q32[OWN[h], s % 2, :]).then_inc(q_hi, 1)

            def hi_k(n, s):
                t = 8 * n + s
                act.wait_ge(k_done, t + 1)
                for h in range(2):
                    nc.scalar.activation(KA[OWN[h], s % 4, h, :], misc[OWN[h], :], ACT.Identity,
                                         bias=bcol[OWN[h], PAIRS + s % PAIRS:PAIRS + s % PAIRS + 1]).then_inc(k_hi, 1)

            def evac_v(group, half, tb, staged):
                act.wait_ge(v_done, group + 1)
                wait(act, d_vs[0], staged[0])
                wait(act, d_vs[1], staged[1])
                nc.scalar.copy(VALL[:, tb, half * L:(half + 1) * L], misc[:, :]).then_inc(v_evac, 1)

            def evac_pv(n, s):
                t = 8 * n + s
                act.wait_ge(pv_done, t + 1)
                if s == 0:
                    wait(act, o_done, n)
                nc.scalar.copy(AT[:, s % PAIRS, :], pv[:, :]).then_inc(pv_evac, 1)

            def exps(n, s, u):
                t = 8 * n + s
                act.wait_ge(st_done, 4 * t + u + 1)
                wait(act, pv_done, t - 1)
                wait(act, sum_done, t - 1)
                kb = 2 * (u // 2)
                nc.scalar.activation(probs[:, s % 2, u % 2, kb:kb + 2, :], st[:, u % 2, :, :], ACT.Exp,
                                     scale=SCALE).then_inc(exp_done, 1)

            act.wait_ge(bias_half, 1)
            act.wait_ge(wl_done, 1)
            act.wait_ge(gw_tr, 2)
            act.wait_ge(xl_done, N)
            for tb in range(TB):
                evac_v(tb, 0, tb, (0, 0))
            for s in range(2):
                evac_q(0, s)
                hi_q(0, s)
                hi_k(0, s)

            def step(n, first, last):
                for s in range(PAIRS):
                    ahead = not (last and s >= 6)
                    if first:
                        hi_state(s)
                    if ahead:
                        evac_q(n, s + 2)
                    if s == 0 and not first:
                        tanh_h(n - 1)
                    if first:
                        tanh_gate(s, 0)
                    exps(n, s, 0)
                    if ahead:
                        hi_k(n, s + 2)
                        hi_q(n, s + 2)
                    if first:
                        tanh_gate(s, 1)
                    exps(n, s, 1)
                    if first:
                        tanh_gate(s, 2)
                    if s < 4:
                        evac_v(4 + 8 * n + s, 1, s, (64 * n, 64 * n))
                    elif not last:
                        evac_v(4 + 8 * n + s, 0, s - 4, (64 * n + 32, 64 * n + 32))
                    exps(n, s, 2)
                    if first and s == 7:
                        act.wait_ge(ab_done, 2 * N)
                    if not (first and s == 0):
                        evac_pv(n - int(s < 1), (s - 1) % PAIRS)
                    exps(n, s, 3)
                if first:
                    hi_state(N)

            batches(act, step)
            evac_pv(N - 1, 7)
            tanh_h(N - 1)

        @block.vector
        def _(dve):
            nc.vector.memset(epst[:, :], EPS).then_inc(eps_set, 1)
            def layernorm(m):
                for k in range(2):
                    n = 2 * m + k
                    for b in range(TB):
                        nc.vector.bn_stats(stats[:, TB * k + b, :], x_all[:, n, b, :]).then_inc(bn_part, 1)
                    for b in range(TB):
                        dve.wait_ge(bn_part, 4 * n + b + 1)
                        if not isinstance(m, int):
                            dve.sem_inc(passed_dve, 1)
                        nc.vector.bn_aggr(mv[:, k, b, :], stats[:, TB * k + b, :]).then_inc(bn_done, 1)
                for k in range(2):
                    n = 2 * m + k
                    dve.wait_ge(std_done, n + 1)
                    nc.vector.reciprocal(rstd[:, k, :], std[:, k, :]).then_inc(rstd_done, 1)
                    dve.wait_ge(rstd_done, n + 1)
                    for b in range(TB):
                        nc.vector.tensor_scalar(xn[:, k, b, :], x_all[:, n, b, :], mv[:, k, b, 0:1],
                                                rstd[:, k, b:b + 1], ALU.subtract, ALU.mult).then_inc(xn_done, 1)
                for k in range(2):
                    n = 2 * m + k
                    dve.wait_ge(xh_done, n + 1)
                    nc.vector.tensor_tensor(XL[:, n, :], st[:, k, 0, :], XH[:, n, :], ALU.subtract).then_inc(xl_done, 1)

            dve.wait_ge(ld_x0, 16)
            layernorm(0)
            dve.wait_ge(ld_x, 16 * (N // 2 - 1))
            with dve.Fori(1, N // 2) as m:
                layernorm(m)
            for k in range(2):
                dve.wait_ge(gw_hi, k + 1)
                nc.vector.scalar_tensor_tensor(gwL[:, 4 * k:4 * k + 4, :],
                                               mx[:, k, :].rearrange("p (w m) -> p w m", m=P), 0.5 if k else 1.0,
                                               gwH[:, 4 * k:4 * k + 4, :], ALU.mult, ALU.subtract).then_inc(gw_lo, 1)
            dve.wait_ge(bias_col, 1)
            nc.vector.tensor_scalar(bhalf[:, :], bcol[:, B_F:B_F + 2], 0.5, None, ALU.mult).then_inc(bias_half, 1)
            dve.wait_ge(bias_fold, 1)
            nc.vector.tensor_tensor(bfin[:, :], misc[:, 0:1], bcol[:, B_OUT:B_OUT + 1], ALU.add).then_inc(bias_fin, 1)
            nc.vector.tensor_scalar(state, bcol[:, IN_C:IN_C + 1].to_broadcast([P, L]), 2.0, None,
                                    ALU.mult).then_inc(state_done, 1)

            def lo_state(step):
                dve.wait_ge(state_hi, step + 1)
                nc.vector.tensor_tensor(DL[:, :], state, DH[:, :], ALU.subtract).then_inc(state_lo, 1)

            def keep(s):
                dve.wait_ge(t_done, 3 * s + 1)
                nc.vector.scalar_tensor_tensor(tf, tf, 1.0, state, ALU.add, ALU.mult).then_inc(ab_done, 1)

            def update(s):
                dve.wait_ge(t_done, 3 * s + 3)
                nc.vector.scalar_tensor_tensor(ti, ti, 1.0, tg, ALU.add, ALU.mult).then_inc(ab_done, 1)
                dve.wait_ge(ab_done, 2 * s + 2)
                nc.vector.scalar_tensor_tensor(state, tf, 0.5, ti, ALU.mult, ALU.add).then_inc(state_done, 1)

            def lo_k(n, s):
                t = 8 * n + s
                for h in range(2):
                    dve.wait_ge(k_hi, 2 * t + h + 1)
                    nc.vector.scalar_tensor_tensor(KA[OTHER[h], s % 4, h, :], misc[OWN[h], :],
                                                   bcol[OWN[h], PAIRS + s % PAIRS:PAIRS + s % PAIRS + 1],
                                                   KA[OWN[h], s % 4, h, :], ALU.add, ALU.subtract).then_inc(k_lo, 1)

            def lo_q(n, s):
                t = 8 * n + s
                wait(dve, st_done, 4 * t - 4)
                for h in range(2):
                    dve.wait_ge(q_hi, 2 * t + h + 1)
                    nc.vector.tensor_tensor(QC[OWN[h], s % 2, h, :], Q32[OWN[h], s % 2, :], QB[OWN[h], s % 4, h, :],
                                            ALU.subtract).then_inc(q_lo, 1)

            def maxima(n, s, js):
                t = 8 * n + s
                for j in js:
                    if j == 0:
                        wait(dve, max_turned, t)
                    dve.wait_ge(mx_done, 8 * t + j + 1)
                    nc.vector.tensor_reduce(NM[:, j:j + 1], mx[:, j % 2, :], AX.X, ALU.max,
                                            negate=True).then_inc(red_done, 1)

            def take_max(n, s):
                t = 8 * n + s
                dve.wait_ge(max_turned, t + 1)
                wait(dve, d_m[(s - 1) % 2], dmas(n, s - 1, 2))
                nc.vector.tensor_copy(TM[:, :], mx[0:2 * TB, 0, 0:P]).then_inc(tm_done, 1)

            def divisors(n, s):
                t = 8 * n + s
                dve.wait_ge(den_done, t + 1)
                wait(dve, norm_done, t)
                nc.vector.transpose(RD[:, :], misc[:, :]).then_inc(den_used, 1)
                dve.wait_ge(den_used, t + 1)
                nc.vector.reciprocal(R16[:, :], RD[:, :].rearrange("p (c j) -> p c j", j=32)[:, :, 0]).then_inc(r16_done, 1)
                dve.wait_ge(r16_done, t + 1)
                nc.vector.transpose(RD[:, :].rearrange("p (c j) -> p c j", j=32),
                                    R16[:, :].unsqueeze(2).to_broadcast([P, L // 32, 32])).then_inc(rd_done, 1)

            def join(n):
                dve.wait_ge(o_done, n + 1)
                dve.wait_ge(ht_done, n + 1)
                nc.vector.scalar_tensor_tensor(OT[:, :], misc[:, :], bfin[:, :], OT[:, :], ALU.add,
                                               ALU.add).then_inc(o_evac, 1)

            def finish(n):
                dve.wait_ge(tr_done, n + 1)
                dve.wait_ge(d_res, 16 * n + 16)
                nc.vector.tensor_tensor(RES[:, :, :], misc[:, :].rearrange("p (b d) -> p b d", d=D), RES[:, :, :],
                                        ALU.add).then_inc(out_done, 1)

            lo_k(0, 0)
            lo_k(0, 1)
            lo_q(0, 0)
            maxima(0, 0, range(8))
            take_max(0, 0)

            def step(n, first, last):
                for s in range(PAIRS):
                    if first:
                        lo_state(s)
                    if not (last and s == 7):
                        maxima(n, s + 1, range(0, 5))
                    if not (last and s >= 6):
                        lo_k(n, s + 2)
                    if not (last and s == 7):
                        maxima(n, s + 1, range(5, 7))
                        if s == 1 and not first:
                            join(n - 1)
                        maxima(n, s + 1, range(7, 8))
                        lo_q(n, s + 1)
                        take_max(n, s + 1)
                    if first:
                        keep(s)
                        update(s)
                    if not (first and s == 0):
                        divisors(n, s - 1)
                    if s == 2 and not first:
                        finish(n - 1)
                if first:
                    lo_state(N)

            batches(dve, step)
            divisors(N - 1, 7)
            join(N - 1)
            finish(N - 1)

        @block.tensor
        def _(pe):
            def product(dst, terms):
                for i, (stationary, moving) in enumerate(terms):
                    last = nc.tensor.matmul(dst, stationary, moving, start=(i == 0), stop=(i == len(terms) - 1))
                return last

            pe.wait_ge(id1, 1)
            pe.wait_ge(ld_b, 16 * 7)
            nc.tensor.transpose(misc[:, 0:BIASES], brow[0:BIASES, :], ident[0:BIASES, 0:BIASES]).then_inc(bias_tr, 1)
            with pe.Fori(0, N // 2) as m:
                for k in range(2):
                    n = 2 * m + k
                    pe.wait_ge(xn_done, 4 * n + 4)
                    for b in range(TB):
                        last = nc.tensor.transpose(st[:, k, 0, b * P:(b + 1) * P], xn[:, k, b, :], ident[:, :])
                    last.then_inc(xt_done, 1)
            pe.wait_ge(ld_w, 16 * 8)
            for k in range(2):
                for i in range(4):
                    last = nc.tensor.transpose(mx[:, k, i * P:(i + 1) * P], w_raw[:, 4 * k + i, :], ident[:, :])
                last.then_inc(gw_tr, 1)
            pe.wait_ge(ld_wo, 16)
            pe.wait_ge(bias_col, 1)
            for c in range(PAIRS):
                last = nc.tensor.matmul(misc[:, 0:1], WO[:, c, :], bcol[:, B_V + c:B_V + c + 1], start=(c == 0),
                                        stop=(c == PAIRS - 1))
            last.then_inc(bias_fold, 1)

            def recurrence(g, n, done, at):
                pe.wait_ge(state_hi, at + 1)
                pe.wait_ge(state_lo, at + 1)
                product(misc[:, :], [(gwH[:, g, :], XH[:, n, :]), (gwL[:, g, :], XH[:, n, :]),
                                     (gwH[:, g, :], XL[:, n, :]), (gwH[:, 4 + g, :], DH[:, :]),
                                     (gwL[:, 4 + g, :], DH[:, :]), (gwH[:, 4 + g, :], DL[:, :])]).then_inc(done, 1)

            def project(n, s, column, done):
                nn = n + s // PAIRS
                c = slice(column + (s % PAIRS) * P, column + (s % PAIRS) * P + P)
                product(misc[:, :], [(WH[:, c], XH[:, nn, :]), (WL[:, c], XH[:, nn, :]),
                                     (WH[:, c], XL[:, nn, :])]).then_inc(done, 1)

            def project_v(half, tb):
                c = slice(2 * DIM + half * L, 2 * DIM + (half + 1) * L)
                b = slice(tb * P, (tb + 1) * P)
                product(misc[:, :], [(XSH[:, b], WH[:, c]), (XSL[:, b], WH[:, c]),
                                     (XSH[:, b], WL[:, c])]).then_inc(v_done, 1)

            def scores_for_max(n, s, js):
                t = 8 * n + s
                for j in js:
                    h, b = j // 4, j % 4
                    if j == 0:
                        pe.wait_ge(d_dup[s % 2], dmas(n, s, 2))
                        pe.wait_ge(k_lo, 2 * t + 2)
                        wait(pe, tm_done, t)
                    wait(pe, red_done, 8 * t + j - 1)
                    nc.tensor.matmul(mx[:, j % 2, :], QB[:, s % 4, h, b * P:(b + 1) * P], KA[:, s % 4, h, :],
                                     start=True, stop=True).then_inc(mx_done, 1)

            def turn_max(n, s):
                t = 8 * n + s
                pe.wait_ge(red_done, 8 * t + 8)
                nc.tensor.transpose(mx[0:2 * TB, 0, 0:P], NM[:, :], ident[:, :]).then_inc(max_turned, 1)

            def scores(n, s, u):
                t = 8 * n + s
                h = u % 2
                if u == 0:
                    pe.wait_ge(d_kc[s % 2], dmas(n, s, 2))
                    pe.wait_ge(d_m[s % 2], dmas(n, s, 2))
                    pe.wait_ge(q_lo, 2 * t + 2)
                wait(pe, exp_done, 4 * t + u - 1)
                for i in range(2):
                    kb = 2 * (u // 2) + i
                    b = slice(kb * P, (kb + 1) * P)
                    nc.tensor.matmul(st[:, h, i, :], KA[:, s % 4, h, b], QB[:, s % 4, h, :], start=True, stop=False)
                    last = nc.tensor.matmul(st[:, h, i, :], KC[:, s % 2, h, b], QC[:, s % 2, h, :], start=False,
                                            stop=True)
                last.then_inc(st_done, 1)

            def values(n, s, kb):
                t = 8 * n + s
                if kb % 2 == 0:
                    pe.wait_ge(exp_done, 4 * t + kb + 2)
                if kb == 0:
                    pe.wait_ge(d_vs[s % 2], dmas(n, s, 1))
                    wait(pe, pv_evac, t)
                for h in range(2):
                    last = nc.tensor.matmul(pv[OWN[h], :], VS[:, s % 2, kb, h * HD:(h + 1) * HD],
                                            probs[:, s % 2, h, kb, :], start=(kb == 0), stop=(kb == TB - 1))
                if kb == TB - 1:
                    last.then_inc(pv_done, 1)

            def sums(n, s):
                t = 8 * n + s
                pe.wait_ge(sum_done, t + 1)
                for h in range(2):
                    last = nc.tensor.matmul(misc[OWN[h], :], ones[:, :], PSUMK[:, h, :], start=True, stop=True)
                last.then_inc(den_done, 1)

            def project_out():
                product(misc[:, :], [(WO[:, c, :], AT[:, c, :]) for c in range(PAIRS)]).then_inc(o_done, 1)

            def turn_out(n):
                pe.wait_ge(o_evac, n + 1)
                for b in range(TB):
                    last = nc.tensor.transpose(misc[:, b * P:(b + 1) * P], OT[:, b * P:(b + 1) * P], ident[:, :])
                last.then_inc(tr_done, 1)

            pe.wait_ge(gw_lo, 2)
            pe.wait_ge(xl_done, N)
            pe.wait_ge(bias_fin, 1)
            pe.wait_ge(wl_done, 1)
            pe.wait_ge(d_xs, 32)
            for tb in range(TB):
                wait(pe, v_evac, tb)
                project_v(0, tb)
            pe.wait_ge(v_evac, TB)
            for s in range(2):
                wait(pe, k_lo, 2 * s)
                project(0, s, 0, q_done)
                pe.wait_ge(q_evac, s + 1)
                project(0, s, DIM, k_done)
            scores_for_max(0, 0, range(8))
            turn_max(0, 0)
            pe.wait_ge(ones_set, 1)
            pe.wait_ge(pads_set, 6)

            def step(n, first, last):
                for s in range(PAIRS):
                    t = 8 * n + s
                    ahead = not (last and s >= 6)
                    behind = not (first and s == 0)

                    def maxima_part(j):
                        if not (last and s == 7):
                            scores_for_max(n, s + 1, (j,))

                    maxima_part(0)
                    if s == 3 and not first:
                        pe.wait_ge(out_done, n)
                    elif first and s == 0:
                        pe.wait_ge(k_lo, 4)
                    elif first and s == 1:
                        pe.wait_ge(t_done, 3)
                    else:
                        pe.wait_ge(den_used, t - 1)
                    if ahead:
                        project(n, s + 2, 0, q_done)
                    maxima_part(1)
                    if behind:
                        values(n, s - 1, 0)
                    if first:
                        pe.wait_ge(q_evac, t + 3)
                        recurrence(0, s, gate_done, s)
                    elif s == 0:
                        pe.wait_ge(q_evac, t + 3)
                        recurrence(3, n - 1, h_done, N)
                    maxima_part(2)
                    scores(n, s, 0)

                    maxima_part(3)
                    if first:
                        pe.wait_ge(t_done, 3 * s + 1)
                    elif s == 0:
                        pe.wait_ge(ht_done, n)
                    elif ahead:
                        pe.wait_ge(q_evac, t + 3)
                    if ahead:
                        project(n, s + 2, DIM, k_done)
                    maxima_part(4)
                    if behind:
                        values(n, s - 1, 1)
                    if first:
                        pe.wait_ge(k_lo, 2 * t + 6)
                        recurrence(1, s, gate_done, s)
                    maxima_part(5)
                    scores(n, s, 1)

                    maxima_part(6)
                    if first:
                        pe.wait_ge(t_done, 3 * s + 2)
                        recurrence(2, s, gate_done, s)
                    if s == 1 and not first:
                        pe.wait_ge(k_lo, 2 * t + 6)
                        pe.wait_ge(norm_done, 8 * n)
                        project_out()
                    if behind:
                        values(n, s - 1, 2)
                    maxima_part(7)
                    if first:
                        pe.wait_ge(t_done, 3 * s + 3)
                    elif s == 1:
                        pe.wait_ge(o_evac, n)
                    elif ahead:
                        pe.wait_ge(k_lo, 2 * t + 6)
                    if s == 4 and not last:
                        pe.wait_ge(d_xs, 32 * n + 64)
                    if s < 4:
                        project_v(1, s)
                    elif not last:
                        project_v(0, s - 4)
                    scores(n, s, 2)

                    if not (last and s == 7):
                        turn_max(n, s + 1)
                    if behind:
                        values(n, s - 1, 3)
                    if s < 4 or not last:
                        pe.wait_ge(v_evac, 4 + t + 1)
                    if behind:
                        sums(n, s - 1)
                    scores(n, s, 3)
                    if s == 2 and not first:
                        pe.wait_ge(den_used, t)
                        turn_out(n - 1)

            batches(pe, step)
            for kb in range(TB):
                values(N - 1, 7, kb)
            pe.wait_ge(den_used, 8 * N - 1)
            sums(N - 1, 7)
            pe.wait_ge(den_used, 8 * N)
            recurrence(3, N - 1, h_done, N)
            pe.wait_ge(ht_done, N)
            pe.wait_ge(norm_done, 8 * N)
            project_out()
            turn_out(N - 1)


_INS = ['L0_attn_data', 'L0_attn_W_qkv', 'L0_attn_b_qkv', 'L0_attn_W_out', 'L0_attn_b_out', 'L0_ffn_wf', 'L0_ffn_uf',
        'L0_ffn_bf', 'L0_ffn_wi', 'L0_ffn_ui', 'L0_ffn_bi', 'L0_ffn_wc', 'L0_ffn_uc', 'L0_ffn_bc', 'L0_ffn_wo',
        'L0_ffn_uo', 'L0_ffn_bo', 'L0_ffn_in_c']


def kernel(**inputs):
    import numpy as _np
    import concourse.bacc as _bacc
    from concourse import mybir as _mybir
    from concourse.bass_utils import run_bass_kernel_spmd as _run

    nc = _bacc.Bacc("TRN2", target_bir_lowering=False, num_devices=1)
    arrays, args = {}, []
    for name in _INS:
        a = _np.ascontiguousarray(inputs[name])
        arrays[f"in_{name}_dram"] = a
        args.append(nc.dram_tensor(f"in_{name}_dram", a.shape, _mybir.dt.from_np(a.dtype), kind="ExternalInput").ap())
    shape = arrays["in_L0_attn_data_dram"].shape
    args.append(nc.dram_tensor("out_dram", shape, _mybir.dt.float32, kind="ExternalOutput").ap())
    build_block(nc, *args)
    r = _run(nc, [arrays], core_ids=[0])
    return r.results[0]["out_dram"]
```

```python
import concourse.bass as bass
from concourse import mybir
from contextlib import ExitStack


def build_block(nc, data, W_qkv, b_qkv, W_out, b_out, wf, uf, bf, wi, ui, bi, wc, uc, bc, wo, uo, bo, in_c, out):
    f32 = mybir.dt.float32
    f32r = mybir.dt.float32r
    ALU = mybir.AluOpType
    ACT = mybir.ActivationFunctionType
    AX = mybir.AxisListType

    P = 128
    N, L, D = data.shape
    DIM = W_qkv.shape[1] // 3
    PAIRS = DIM // P
    HD = P // 2
    TB = L // P
    SCALE = float(HD) ** -0.5
    EPS = 1e-5
    HALVES = 2
    BIASES = 3 * PAIRS + 6
    B_V, B_OUT, B_F, B_I, B_C, B_O, IN_C = 2 * PAIRS, 3 * PAIRS, 25, 26, 27, 28, 29
    OWN = [slice(0, HD), slice(HD, P)]
    OTHER = [slice(HD, P), slice(0, HD)]
    AUX = [slice(HD, HD + 1), slice(0, 1)]

    W_PARTS = (2, 0, 1)

    data_t = data.rearrange("n (b p) d -> p n b d", p=P)
    out_t = out.rearrange("n (b p) d -> p n b d", p=P)
    Wo_v = W_out.rearrange("(c p) d -> p c d", p=P)

    ctx = ExitStack()
    with ctx:
        def sb(name, shape, dt=f32):
            return ctx.enter_context(nc.sbuf_tensor(name, shape, dt))

        def sem(name):
            return ctx.enter_context(nc.semaphore(name))

        ident = sb("ident", [P, P])
        ones = sb("ones", [P, HD])
        bcol = sb("bcol", [P, 32])
        bhalf = sb("bhalf", [P, 2])
        bfin = sb("bfin", [P, 1])
        probs = sb("probs", [P, 2, 2, TB, L])
        XH = sb("XH", [P, N, L], f32r)
        XL = sb("XL", [P, N, L], f32r)
        WH = sb("WH", [P, 3 * DIM], f32r)
        WL = sb("WL", [P, 3 * DIM], f32r)
        WO = sb("WO", [P, PAIRS, D])
        VALL = sb("VALL", [P, TB, DIM])
        XSH = sb("XSH", [P, L], f32r)
        XSL = sb("XSL", [P, L], f32r)
        VS = sb("VS", [P, 2, TB, P])
        Q32 = sb("Q32", [P, 2, L])
        QB = sb("QB", [P, 4, 2, L], f32r)
        KA = sb("KA", [P, 4, 2, L], f32r)
        QC = sb("QC", [P, 2, 2, L], f32r)
        KC = sb("KC", [P, 2, 2, L], f32r)
        PSUMK = sb("PSUMK", [P, 2, L])
        R16 = sb("R16", [P, L // 32])
        RD = sb("RD", [P, L])
        AT = sb("AT", [P, PAIRS, L])
        OT = sb("OT", [P, L])
        RES = sb("RES", [P, TB, D])
        gwH = sb("gwH", [P, 8, P], f32r)
        gwL = sb("gwL", [P, 8, P], f32r)
        DH = sb("DH", [P, L], f32r)
        DL = sb("DL", [P, L], f32r)
        NM = sb("NM", [P, 2 * TB])
        TM = sb("TM", [2 * TB, P])
        epst = sb("epst", [P, 1])

        x_all = probs[:, 1, :, :, :].rearrange("p a b l -> p (a b l)").rearrange("p (n b d) -> p n b d", n=N, d=D)
        rest = probs[:, 0, :, :, :].rearrange("p a b l -> p (a b l)")
        W_raw = rest[:, 0:3 * DIM]
        w_raw = rest[:, 3 * DIM:3 * DIM + 8 * P].rearrange("p (w i) -> p w i", w=8)
        xn = [AT[:, a, :].rearrange("p (b d) -> p b d", d=D) for a in (0, 1, 5, 6)]
        brow = AT[0:32, 2, 0:P]
        stats = AT[:, 3, 0:6 * N * TB].rearrange("p (n b c) -> p n b c", b=TB, c=6)
        mv = AT[:, 4, 0:2 * N * TB].rearrange("p (n b c) -> p n b c", b=TB, c=2)
        std = AT[:, 4, 2 * P:2 * P + N * TB].rearrange("p (n b) -> p n b", b=TB)
        rstd = AT[:, 4, 3 * P:3 * P + N * TB].rearrange("p (n b) -> p n b", b=TB)
        state, tf, ti, tg = OT[:, :], RES[:, :, :].rearrange("p b d -> p (b d)"), AT[:, 7, :], AT[:, 6, :]

        st = ctx.enter_context(nc.psum_tensor("st", [P, 2, 2, L], f32))
        mx = ctx.enter_context(nc.psum_tensor("mx", [P, 2, L], f32))
        pv = ctx.enter_context(nc.psum_tensor("pv", [P, L], f32))
        misc = ctx.enter_context(nc.psum_tensor("misc", [P, L], f32))

        first_v = [st[:, tb // 2, tb % 2, :] for tb in range(TB)]
        first_q, first_k = [pv[:, :], st[:, 0, 0, :]], [misc[:, :], st[:, 0, 1, :]]

        x_banks = [mx[:, 0, :], mx[:, 1, :]] + [st[:, 1, 0, :], st[:, 1, 1, :], pv[:, :], misc[:, :]] * 2

        w_banks = [st[:, 0, 1, :], st[:, 0, 0, :]]

        passed_sp = sem("passed_sp")
        ld_x0 = sem("ld_x0")
        ld_b, ld_x, ld_w, ld_wo = sem("ld_b"), sem("ld_x"), sem("ld_w"), sem("ld_wo")
        ld_W = [sem("ld_Wq"), sem("ld_Wk"), sem("ld_Wv")]
        id0, id1, ones_set, pads_set, eps_set = sem("id0"), sem("id1"), sem("ones_set"), sem("pads_set"), sem("eps_set")
        bias_tr, bias_col, bias_half, bias_fold, bias_fin = (sem("bias_tr"), sem("bias_col"), sem("bias_half"),
                                                             sem("bias_fold"), sem("bias_fin"))
        gw_tr, gw_hi, gw_lo = sem("gw_tr"), sem("gw_hi"), sem("gw_lo")
        bn_part, bn_done, std_done, rstd_done, xn_done, xt_done, xh_done, xl_done = (
            sem("bn_part"), sem("bn_done"), sem("std_done"), sem("rstd_done"), sem("xn_done"), sem("xt_done"),
            sem("xh_done"), sem("xl_done"))
        wh_done, wl_done = sem("wh_done"), sem("wl_done")
        state_done, state_hi, state_lo, gate_done, t_done, ab_done, h_done, ht_done = (
            sem("state_done"), sem("state_hi"), sem("state_lo"), sem("gate_done"), sem("t_done"), sem("ab_done"),
            sem("h_done"), sem("ht_done"))
        q_done, k_done, v_done, den_done, o_done, tr_done = (
            sem("q_done"), sem("k_done"), sem("v_done"), sem("den_done"), sem("o_done"), sem("tr_done"))
        st_done, mx_done, pv_done = sem("st_done"), sem("mx_done"), sem("pv_done")
        q_evac, v_evac, q_hi, k_hi, exp_done, pv_evac, o_evac = (
            sem("q_evac"), sem("v_evac"), sem("q_hi"), sem("k_hi"), sem("exp_done"),
            sem("pv_evac"), sem("o_evac"))
        q_lo, k_lo, red_done, max_turned, tm_done, den_used, r16_done, rd_done, out_done = (
            sem("q_lo"), sem("k_lo"), sem("red_done"), sem("max_turned"), sem("tm_done"), sem("den_used"), sem("r16_done"),
            sem("rd_done"), sem("out_done"))
        sum_part, sum_done, norm_done = sem("sum_part"), sem("sum_done"), sem("norm_done")
        d_dup = [sem("d_dup0"), sem("d_dup1")]
        d_kc = [sem("d_kc0"), sem("d_kc1")]
        d_m = [sem("d_m0"), sem("d_m1")]
        d_vs = [sem("d_vs0"), sem("d_vs1")]
        d_xs, d_res, out_rows = sem("d_xs"), sem("d_res"), sem("out_rows")

        def wait(eng, s, value):
            if not (isinstance(value, int) and value <= 0):
                eng.wait_ge(s, value)

        def dmas(n, s, each):
            return (4 * n + s // 2 + 1) * (16 * each)

        def batches(eng, step):
            step(0, True, False)
            with eng.Fori(1, N - 1) as n:
                step(n, False, False)
            step(N - 1, False, True)

        block = ctx.enter_context(nc.Block())

        @block.sync
        def _(sp):
            sp.dma_start(x_all[:, 0:2, :, :], data_t[:, 0:2, :, :]).then_inc(ld_x0, 16)
            sp.dma_start(brow[0:3 * PAIRS, :], b_qkv.rearrange("(c r) -> c r", r=P)).then_inc(ld_b, 16)
            for i, v in enumerate((b_out, bf, bi, bc, bo, in_c)):
                sp.dma_start(brow[B_OUT + i:B_OUT + i + 1, :], v.rearrange("(a r) -> a r", a=1)).then_inc(ld_b, 16)
            for i in W_PARTS:
                sp.dma_start(W_raw[:, i * DIM:(i + 1) * DIM], W_qkv[:, i * DIM:(i + 1) * DIM]).then_inc(ld_W[i], 16)
            for n in range(2, N, 2):
                sp.dma_start(x_all[:, n:n + 2, :, :], data_t[:, n:n + 2, :, :]).then_inc(ld_x, 16)
            for i, w in enumerate((wf, wi, wc, wo, uf, ui, uc, uo)):
                sp.dma_start(w_raw[:, i, :], w).then_inc(ld_w, 16)
            sp.dma_start(WO[:, :, :], Wo_v).then_inc(ld_wo, 16)

            def stage_x(n):
                sp.wait_ge(xl_done, 1 if isinstance(n, int) and n == 0 else N)
                sp.dma_start(XSH[:, :].bitcast(f32), XH[:, n, :].bitcast(f32)).then_inc(d_xs, 16)
                sp.dma_start(XSL[:, :].bitcast(f32), XL[:, n, :].bitcast(f32)).then_inc(d_xs, 16)

            def duplicate_q(n, s):
                t = 8 * n + s
                sp.wait_ge(q_hi, 2 * t + 2)
                sp.sem_inc(passed_sp, 1)
                for h in range(2):
                    sp.dma_start(QB[OTHER[h], s % 4, h, :].bitcast(f32), QB[OWN[h], s % 4, h, :].bitcast(f32)).then_inc(d_dup[s % 2], 16)

            def copy_k(n, s):
                t = 8 * n + s
                wait(sp, st_done, 4 * t - 4)
                sp.sem_inc(passed_sp, 1)
                sp.wait_ge(k_hi, 2 * t + 2)
                sp.sem_inc(passed_sp, 1)
                for h in range(2):
                    sp.dma_start(KC[OWN[h], s % 2, h, :].bitcast(f32), KA[OWN[h], s % 4, h, :].bitcast(f32)).then_inc(d_kc[s % 2], 16)

            def place_max(n, s):
                t = 8 * n + s
                sp.wait_ge(tm_done, t + 1)
                sp.sem_inc(passed_sp, 1)
                for h in range(2):
                    sp.dma_start(QC[AUX[h], s % 2, h, :].bitcast(f32).rearrange("p (b j) -> p b j", j=P),
                                 TM[TB * h:TB * h + TB, :]).then_inc(d_m[s % 2], 16)

            stage_x(0)
            sp.wait_ge(pads_set, 6)
            duplicate_q(0, 0)
            copy_k(0, 0)
            duplicate_q(0, 1)
            place_max(0, 0)

            def step(n, first, last):
                for s in range(PAIRS):
                    t = 8 * n + s
                    if not (last and s == 7):
                        copy_k(n, s + 1)
                    sp.wait_ge(v_evac, 8 * n + (4 if s < 4 else 8))
                    sp.sem_inc(passed_sp, 1)
                    wait(sp, pv_done, t - 1)
                    sp.sem_inc(passed_sp, 1)
                    sp.dma_start(VS[:, s % 2, :, :], VALL[:, :, s * P:(s + 1) * P]).then_inc(d_vs[s % 2], 16)
                    if s == 0 and not first:
                        sp.wait_ge(state_lo, N + 1)
                        sp.dma_start(RES[:, :, :], data_t[:, n - 1, :, :]).then_inc(d_res, 16)
                    if s == 3 and not first:
                        sp.wait_ge(out_done, n)
                        sp.sem_inc(passed_sp, 1)
                        sp.dma_start(out_t[:, n - 1, :, :], RES[:, :, :]).then_inc(out_rows, 16)
                    if s == 7 and not first:
                        sp.wait_ge(out_rows, 16 * n)
                        sp.sem_inc(passed_sp, 1)
                    if s == 4 and not last:
                        sp.wait_ge(v_done, 8 * n + 8)
                        sp.sem_inc(passed_sp, 1)
                        stage_x(n + 1)
                    if not (last and s >= 6):
                        duplicate_q(n, s + 2)
                    if not (last and s == 7):
                        place_max(n, s + 1)

            batches(sp, step)
            sp.dma_start(RES[:, :, :], data_t[:, N - 1, :, :]).then_inc(d_res, 16)
            sp.wait_ge(out_done, N)
            sp.dma_start(out_t[:, N - 1, :, :], RES[:, :, :]).then_inc(out_rows, 16)
            sp.wait_ge(out_rows, 16 * N)

        @block.gpsimd
        def _(pool):
            nc.gpsimd.memset(ident[:, :], 0.0).then_inc(id0, 1)
            pool.wait_ge(id0, 1)
            nc.gpsimd.affine_select(out=ident[:, :], in_=ident[:, :], compare_op=ALU.not_equal, fill=1.0, base=0,
                                    pattern=[[-1, P]], channel_multiplier=1).then_inc(id1, 1)
            nc.gpsimd.memset(ones[:, :], 1.0).then_inc(ones_set, 1)
            pool.wait_ge(ones_set, 1)
            for h in range(2):
                nc.gpsimd.memset(KC[OTHER[h], :, h, :].bitcast(f32), 0.0).then_inc(pads_set, 1)
                pool.wait_ge(pads_set, 3 * h + 1)
                nc.gpsimd.memset(QC[OTHER[h], :, h, :].bitcast(f32), 0.0).then_inc(pads_set, 1)
                pool.wait_ge(pads_set, 3 * h + 2)
                nc.gpsimd.memset(KC[AUX[h], :, h, :].bitcast(f32), 1.0).then_inc(pads_set, 1)
                pool.wait_ge(pads_set, 3 * h + 3)

            def lo_weights(order):
                i = W_PARTS[order]
                pool.wait_ge(wh_done, order + 1)
                nc.gpsimd.tensor_tensor(WL[:, i * DIM:(i + 1) * DIM], W_raw[:, i * DIM:(i + 1) * DIM],
                                        WH[:, i * DIM:(i + 1) * DIM], ALU.subtract).then_inc(wl_done, 1)

            for order in range(3):
                lo_weights(order)

            def normalise(n, s):
                t = 8 * n + s
                pool.wait_ge(rd_done, t + 1)
                pool.wait_ge(pv_evac, t + 1)
                nc.gpsimd.tensor_tensor(AT[:, s % PAIRS, :], AT[:, s % PAIRS, :], RD[:, :], ALU.mult).then_inc(norm_done, 1)

            def sum_blocks(n, s):
                t = 8 * n + s
                pool.wait_ge(exp_done, 4 * t + 2)
                wait(pool, den_done, t)
                e = probs[:, s % 2, :, :, :]
                nc.gpsimd.tensor_tensor(PSUMK[:, :, :], e[:, :, 0, :], e[:, :, 1, :], ALU.add).then_inc(sum_part, 1)
                pool.wait_ge(exp_done, 4 * t + 4)
                pool.wait_ge(sum_part, 2 * t + 1)
                nc.gpsimd.tensor_tensor(PSUMK[:, :, :], PSUMK[:, :, :], e[:, :, 2, :], ALU.add).then_inc(sum_part, 1)
                pool.wait_ge(sum_part, 2 * t + 2)
                nc.gpsimd.tensor_tensor(PSUMK[:, :, :], PSUMK[:, :, :], e[:, :, 3, :], ALU.add).then_inc(sum_done, 1)

            def step(n, first, last):
                for s in range(PAIRS):
                    if not (first and s == 0):
                        sum_blocks(n - int(s < 1), (s - 1) % PAIRS)
                    if not (first and s == 0):
                        normalise(n - int(s < 1), (s - 1) % PAIRS)

            batches(pool, step)
            normalise(N - 1, 7)

        @block.scalar
        def _(act):
            act.wait_ge(bias_tr, 1)
            nc.scalar.copy(bcol[:, 0:BIASES], misc[:, 0:BIASES]).then_inc(bias_col, 1)

            def deviation(n0, n1):
                act.wait_ge(bn_done, TB * n1)
                act.wait_ge(eps_set, 1)
                nc.scalar.activation(std[:, n0:n1, :], mv[:, n0:n1, :, 1], ACT.Sqrt, bias=epst[:, :]).then_inc(std_done, 1)

            def hi_x(n):
                act.wait_ge(xt_done, n + 1)
                nc.scalar.copy(XH[:, n, :], x_banks[n]).then_inc(xh_done, 1)

            def hi_weights(order):
                i = W_PARTS[order]
                act.wait_ge(ld_W[i], 16)
                nc.scalar.copy(WH[:, i * DIM:(i + 1) * DIM], W_raw[:, i * DIM:(i + 1) * DIM]).then_inc(wh_done, 1)

            def tanh_gate(s, g):
                act.wait_ge(gate_done, 3 * s + g + 1)
                nc.scalar.activation((tf, ti, tg)[g], misc[:, :], ACT.Tanh,
                                     bias=bcol[:, B_C:B_C + 1] if g == 2 else bhalf[:, g:g + 1],
                                     scale=1.0 if g == 2 else 0.5).then_inc(t_done, 1)

            def hi_state(step):
                act.wait_ge(state_done, step + 1)
                nc.scalar.copy(DH[:, :], state).then_inc(state_hi, 1)

            def tanh_h(n, source=misc):
                act.wait_ge(h_done, n + 1)
                nc.scalar.activation(OT[:, :], source[:, :], ACT.Tanh, bias=bcol[:, B_O:B_O + 1]).then_inc(ht_done, 1)

            def evac_q(n, s, source=misc):
                t = 8 * n + s
                act.wait_ge(q_done, t + 1)
                wait(act, q_lo, 2 * t - 2)
                nc.scalar.activation(Q32[:, s % 2, :], source[:, :], ACT.Identity,
                                     bias=bcol[:, s % PAIRS:s % PAIRS + 1]).then_inc(q_evac, 1)

            def hi_q(n, s):
                t = 8 * n + s
                wait(act, st_done, 4 * t - 12)
                act.wait_ge(q_evac, t + 1)
                for h in range(2):
                    nc.scalar.copy(QB[OWN[h], s % 4, h, :], Q32[OWN[h], s % 2, :]).then_inc(q_hi, 1)

            def hi_k(n, s, source=misc):
                t = 8 * n + s
                act.wait_ge(k_done, t + 1)
                for h in range(2):
                    nc.scalar.activation(KA[OWN[h], s % 4, h, :], source[OWN[h], :], ACT.Identity,
                                         bias=bcol[OWN[h], PAIRS + s % PAIRS:PAIRS + s % PAIRS + 1]).then_inc(k_hi, 1)

            def evac_v(group, half, tb, staged, source=misc):
                act.wait_ge(v_done, group + 1)
                wait(act, d_vs[0], staged[0])
                wait(act, d_vs[1], staged[1])
                nc.scalar.copy(VALL[:, tb, half * L:(half + 1) * L], source[:, :]).then_inc(v_evac, 1)

            def evac_pv(n, s):
                t = 8 * n + s
                act.wait_ge(pv_done, t + 1)
                if s == 0:
                    wait(act, o_done, n)
                nc.scalar.copy(AT[:, s % PAIRS, :], pv[:, :]).then_inc(pv_evac, 1)

            def exps(n, s, u):
                t = 8 * n + s
                act.wait_ge(st_done, 4 * t + u + 1)
                wait(act, pv_done, t - 1)
                wait(act, sum_done, t - 1)
                kb = 2 * (u // 2)
                nc.scalar.activation(probs[:, s % 2, u % 2, kb:kb + 2, :], st[:, u % 2, :, :], ACT.Exp,
                                     scale=SCALE).then_inc(exp_done, 1)

            deviation(0, 2)
            hi_weights(0)
            hi_x(0)
            hi_x(1)
            hi_weights(1)
            hi_weights(2)
            for tb in range(TB):
                evac_v(tb, 0, tb, (0, 0), first_v[tb])
            deviation(2, N)
            for s in range(2):
                evac_q(0, s, first_q[s])
                hi_q(0, s)
                hi_k(0, s, first_k[s])
            for n in range(2, N):
                hi_x(n)
                if n >= 6:
                    k = n - 6
                    act.wait_ge(gw_tr, k + 1)
                    nc.scalar.mul(gwH[:, 4 * k:4 * k + 4, :], w_banks[k].rearrange("p (w m) -> p w m", m=P),
                                  0.5 if k else 1.0).then_inc(gw_hi, 1)
            act.wait_ge(bias_half, 1)
            act.wait_ge(wl_done, 3)
            act.wait_ge(gw_tr, 2)
            act.wait_ge(xn_done, TB * N)

            def step(n, first, last):
                for s in range(PAIRS):
                    ahead = not (last and s >= 6)
                    if first:
                        hi_state(s)
                    if ahead:
                        evac_q(n, s + 2)
                    if s == 0 and not first:
                        tanh_h(n - 1)
                    if first:
                        tanh_gate(s, 0)
                    exps(n, s, 0)
                    if ahead:
                        hi_k(n, s + 2)
                        hi_q(n, s + 2)
                    exps(n, s, 1)
                    if first:
                        tanh_gate(s, 1)
                        tanh_gate(s, 2)
                        exps(n, s, 2)
                    if s < 4:
                        evac_v(4 + 8 * n + s, 1, s, (64 * n, 64 * n))
                    elif not last:
                        evac_v(4 + 8 * n + s, 0, s - 4, (64 * n + 32, 64 * n + 32))
                    if not first:
                        exps(n, s, 2)
                    if first and s == 7:
                        act.wait_ge(ab_done, 2 * N)
                    if not (first and s == 0):
                        evac_pv(n - int(s < 1), (s - 1) % PAIRS)
                    exps(n, s, 3)
                    if last and s == 7:
                        tanh_h(N - 1, mx[:, 1, :])
                if first:
                    hi_state(N)

            batches(act, step)
            evac_pv(N - 1, 7)

        @block.vector
        def _(dve):
            nc.vector.memset(epst[:, :], EPS).then_inc(eps_set, 1)
            def moments(m):
                for k in range(2):
                    n = 2 * m + k
                    for b in range(TB):
                        nc.vector.bn_stats(stats[:, n, b, :], x_all[:, n, b, :]).then_inc(bn_part, 1)
                for k in range(2):
                    n = 2 * m + k
                    for b in range(TB):
                        dve.wait_ge(bn_part, TB * n + b + 1)
                        nc.vector.bn_aggr(mv[:, n, b, :], stats[:, n, b, :]).then_inc(bn_done, 1)

            def inverse_deviation(count, n0, n1):
                dve.wait_ge(std_done, count)
                nc.vector.reciprocal(rstd[:, n0:n1, :], std[:, n0:n1, :]).then_inc(rstd_done, 1)

            def standardise(n):
                dve.wait_ge(rstd_done, 1 if n < 2 else 2)
                wait(dve, xt_done, n - 3)
                for b in range(TB):
                    nc.vector.tensor_scalar(xn[n % 4][:, b, :], x_all[:, n, b, :], mv[:, n, b, 0:1], rstd[:, n, b:b + 1],
                                            ALU.subtract, ALU.mult).then_inc(xn_done, 1)

            def lo_x(n):
                dve.wait_ge(xh_done, n + 1)
                nc.vector.tensor_tensor(XL[:, n, :], x_banks[n], XH[:, n, :], ALU.subtract).then_inc(xl_done, 1)

            def lo_state(step):
                dve.wait_ge(state_hi, step + 1)
                nc.vector.tensor_tensor(DL[:, :], state, DH[:, :], ALU.subtract).then_inc(state_lo, 1)

            def keep(s):
                dve.wait_ge(t_done, 3 * s + 1)
                nc.vector.scalar_tensor_tensor(tf, tf, 1.0, state, ALU.add, ALU.mult).then_inc(ab_done, 1)

            def update(s):
                dve.wait_ge(t_done, 3 * s + 3)
                nc.vector.scalar_tensor_tensor(ti, ti, 1.0, tg, ALU.add, ALU.mult).then_inc(ab_done, 1)
                dve.wait_ge(ab_done, 2 * s + 2)
                nc.vector.scalar_tensor_tensor(state, tf, 0.5, ti, ALU.mult, ALU.add).then_inc(state_done, 1)

            def lo_k(n, s, source=misc):
                t = 8 * n + s
                for h in range(2):
                    dve.wait_ge(k_hi, 2 * t + h + 1)
                    nc.vector.scalar_tensor_tensor(KA[OTHER[h], s % 4, h, :], source[OWN[h], :],
                                                   bcol[OWN[h], PAIRS + s % PAIRS:PAIRS + s % PAIRS + 1],
                                                   KA[OWN[h], s % 4, h, :], ALU.add, ALU.subtract).then_inc(k_lo, 1)

            def lo_q(n, s):
                t = 8 * n + s
                wait(dve, st_done, 4 * t - 4)
                for h in range(2):
                    dve.wait_ge(q_hi, 2 * t + h + 1)
                    nc.vector.tensor_tensor(QC[OWN[h], s % 2, h, :], Q32[OWN[h], s % 2, :], QB[OWN[h], s % 4, h, :],
                                            ALU.subtract).then_inc(q_lo, 1)

            def maxima(n, s, js):
                t = 8 * n + s
                for j in js:
                    if j == 0:
                        wait(dve, max_turned, t)
                    dve.wait_ge(mx_done, 8 * t + j + 1)
                    nc.vector.tensor_reduce(NM[:, j:j + 1], mx[:, j % 2, :], AX.X, ALU.max,
                                            negate=True).then_inc(red_done, 1)

            def take_max(n, s):
                t = 8 * n + s
                dve.wait_ge(max_turned, t + 1)
                wait(dve, d_m[(s - 1) % 2], dmas(n, s - 1, 2))
                nc.vector.tensor_copy(TM[:, :], mx[0:2 * TB, 0, 0:P]).then_inc(tm_done, 1)

            def divisors(n, s):
                t = 8 * n + s
                dve.wait_ge(den_done, t + 1)
                wait(dve, norm_done, t)
                nc.vector.transpose(RD[:, :], misc[:, :]).then_inc(den_used, 1)
                dve.wait_ge(den_used, t + 1)
                nc.vector.reciprocal(R16[:, :], RD[:, :].rearrange("p (c j) -> p c j", j=32)[:, :, 0]).then_inc(r16_done, 1)
                dve.wait_ge(r16_done, t + 1)
                nc.vector.transpose(RD[:, :].rearrange("p (c j) -> p c j", j=32),
                                    R16[:, :].unsqueeze(2).to_broadcast([P, L // 32, 32])).then_inc(rd_done, 1)

            def join(n, source=misc):
                dve.wait_ge(o_done, n + 1)
                dve.wait_ge(ht_done, n + 1)
                nc.vector.scalar_tensor_tensor(OT[:, :], source[:, :], bfin[:, :], OT[:, :], ALU.add,
                                               ALU.add).then_inc(o_evac, 1)

            def finish(n):
                dve.wait_ge(tr_done, n + 1)
                dve.wait_ge(d_res, 16 * n + 16)
                nc.vector.tensor_tensor(RES[:, :, :], pv[:, :].rearrange("p (b d) -> p b d", d=D), RES[:, :, :],
                                        ALU.add).then_inc(out_done, 1)

            def lo_gates(k):
                dve.wait_ge(gw_hi, k + 1)
                nc.vector.scalar_tensor_tensor(gwL[:, 4 * k:4 * k + 4, :],
                                               w_banks[k].rearrange("p (w m) -> p w m", m=P), 0.5 if k else 1.0,
                                               gwH[:, 4 * k:4 * k + 4, :], ALU.mult, ALU.subtract).then_inc(gw_lo, 1)

            dve.wait_ge(ld_x0, 16)
            moments(0)
            inverse_deviation(1, 0, 2)
            standardise(0)
            standardise(1)
            lo_x(0)
            lo_x(1)
            dve.wait_ge(bias_col, 1)
            nc.vector.tensor_scalar(bhalf[:, :], bcol[:, B_F:B_F + 2], 0.5, None, ALU.mult).then_inc(bias_half, 1)
            nc.vector.tensor_scalar(state, bcol[:, IN_C:IN_C + 1].to_broadcast([P, L]), 2.0, None,
                                    ALU.mult).then_inc(state_done, 1)
            dve.wait_ge(ld_x, 16 * (N // 2 - 1))
            for m in range(1, N // 2):
                moments(m)
            inverse_deviation(2, 2, N)
            for n in range(2, 6):
                standardise(n)
            for s in range(2):
                lo_k(0, s, first_k[s])
            for n in range(2, N):
                lo_x(n)
                if n + 4 < N:
                    standardise(n + 4)
                if n < 6:
                    maxima(0, 0, (2 * n - 4, 2 * n - 3))
                if n == 2:
                    dve.wait_ge(bias_fold, 1)
                    nc.vector.tensor_tensor(bfin[:, :], st[:, 0, 0, 0:1], bcol[:, B_OUT:B_OUT + 1],
                                            ALU.add).then_inc(bias_fin, 1)
                if n == 5:
                    lo_gates(0)
                if n == 6:
                    take_max(0, 0)
            lo_q(0, 0)
            lo_gates(1)

            def step(n, first, last):
                for s in range(PAIRS):
                    if first:
                        lo_state(s)
                    if not (last and s == 7):
                        maxima(n, s + 1, range(0, 5))
                    if not (last and s >= 6):
                        lo_k(n, s + 2)
                    if not (last and s == 7):
                        maxima(n, s + 1, range(5, 7))
                        if s == 1 and not first:
                            join(n - 1)
                        maxima(n, s + 1, range(7, 8))
                        lo_q(n, s + 1)
                        take_max(n, s + 1)
                    if first:
                        keep(s)
                        update(s)
                    if not (first and s == 0):
                        divisors(n, s - 1)
                    if s == 2 and not first:
                        finish(n - 1)
                if first:
                    lo_state(N)

            batches(dve, step)
            divisors(N - 1, 7)
            join(N - 1, mx[:, 0, :])
            finish(N - 1)

        @block.tensor
        def _(pe):
            def product(dst, terms):
                for i, (stationary, moving) in enumerate(terms):
                    last = nc.tensor.matmul(dst, stationary, moving, start=(i == 0), stop=(i == len(terms) - 1))
                return last

            pe.wait_ge(id1, 1)
            pe.wait_ge(ld_b, 16 * 7)
            nc.tensor.transpose(misc[:, 0:BIASES], brow[0:BIASES, :], ident[0:BIASES, 0:BIASES]).then_inc(bias_tr, 1)

            def turn_x(n):
                pe.wait_ge(xn_done, TB * n + TB)
                if n == 2:
                    pe.wait_ge(v_evac, TB)
                if n == 4:
                    pe.wait_ge(q_evac, 1)
                if n == 5:
                    pe.wait_ge(k_lo, 2)
                if n >= 6:
                    pe.wait_ge(xl_done, n - 3)
                for b in range(TB):
                    last = nc.tensor.transpose(x_banks[n][:, b * P:(b + 1) * P], xn[n % 4][:, b, :], ident[:, :])
                last.then_inc(xt_done, 1)

            def recurrence(g, n, done, at, dst=misc):
                pe.wait_ge(state_hi, at + 1)
                pe.wait_ge(state_lo, at + 1)
                product(dst[:, :], [(gwH[:, g, :], XH[:, n, :]), (gwL[:, g, :], XH[:, n, :]),
                                     (gwH[:, g, :], XL[:, n, :]), (gwH[:, 4 + g, :], DH[:, :]),
                                     (gwL[:, 4 + g, :], DH[:, :]), (gwH[:, 4 + g, :], DL[:, :])]).then_inc(done, 1)

            def project(n, s, column, done, dst=misc):
                nn = n + s // PAIRS
                c = slice(column + (s % PAIRS) * P, column + (s % PAIRS) * P + P)
                product(dst[:, :], [(WH[:, c], XH[:, nn, :]), (WL[:, c], XH[:, nn, :]),
                                     (WH[:, c], XL[:, nn, :])]).then_inc(done, 1)

            def project_v(half, tb, hi=XSH, lo=XSL, dst=misc):
                c = slice(2 * DIM + half * L, 2 * DIM + (half + 1) * L)
                b = slice(tb * P, (tb + 1) * P)
                product(dst[:, :], [(hi[:, b], WH[:, c]), (lo[:, b], WH[:, c]),
                                    (hi[:, b], WL[:, c])]).then_inc(v_done, 1)

            def scores_for_max(n, s, js):
                t = 8 * n + s
                for j in js:
                    h, b = j // 4, j % 4
                    if j == 0:
                        pe.wait_ge(d_dup[s % 2], dmas(n, s, 2))
                        pe.wait_ge(k_lo, 2 * t + 2)
                        wait(pe, tm_done, t)
                    wait(pe, red_done, 8 * t + j - 1)
                    nc.tensor.matmul(mx[:, j % 2, :], QB[:, s % 4, h, b * P:(b + 1) * P], KA[:, s % 4, h, :],
                                     start=True, stop=True).then_inc(mx_done, 1)

            def turn_max(n, s):
                t = 8 * n + s
                pe.wait_ge(red_done, 8 * t + 8)
                nc.tensor.transpose(mx[0:2 * TB, 0, 0:P], NM[:, :], ident[:, :]).then_inc(max_turned, 1)

            def scores(n, s, u):
                t = 8 * n + s
                h = u % 2
                if u == 0:
                    pe.wait_ge(d_kc[s % 2], dmas(n, s, 2))
                    pe.wait_ge(d_m[s % 2], dmas(n, s, 2))
                    pe.wait_ge(q_lo, 2 * t + 2)
                wait(pe, exp_done, 4 * t + u - 1)
                for i in range(2):
                    kb = 2 * (u // 2) + i
                    b = slice(kb * P, (kb + 1) * P)
                    nc.tensor.matmul(st[:, h, i, :], KA[:, s % 4, h, b], QB[:, s % 4, h, :], start=True, stop=False)
                    last = nc.tensor.matmul(st[:, h, i, :], KC[:, s % 2, h, b], QC[:, s % 2, h, :], start=False,
                                            stop=True)
                last.then_inc(st_done, 1)

            def values(n, s, kb):
                t = 8 * n + s
                if kb % 2 == 0:
                    pe.wait_ge(exp_done, 4 * t + kb + 2)
                if kb == 0:
                    pe.wait_ge(d_vs[s % 2], dmas(n, s, 1))
                    wait(pe, pv_evac, t)
                    if s == 2 and not (isinstance(n, int) and n == 0):
                        pe.wait_ge(out_done, n)
                for h in range(2):
                    last = nc.tensor.matmul(pv[OWN[h], :], VS[:, s % 2, kb, h * HD:(h + 1) * HD],
                                            probs[:, s % 2, h, kb, :], start=(kb == 0), stop=(kb == TB - 1))
                if kb == TB - 1:
                    last.then_inc(pv_done, 1)

            def sums(n, s):
                t = 8 * n + s
                pe.wait_ge(sum_done, t + 1)
                for h in range(2):
                    last = nc.tensor.matmul(misc[OWN[h], :], ones[:, :], PSUMK[:, h, :], start=True, stop=True)
                last.then_inc(den_done, 1)

            def project_out(dst=misc, pairs=range(PAIRS)):
                for c in pairs:
                    last = nc.tensor.matmul(dst[:, :], WO[:, c, :], AT[:, c, :], start=(c == 0), stop=(c == PAIRS - 1))
                if c == PAIRS - 1:
                    last.then_inc(o_done, 1)

            def turn_out(n):
                pe.wait_ge(o_evac, n + 1)
                for b in range(TB):
                    last = nc.tensor.transpose(pv[:, b * P:(b + 1) * P], OT[:, b * P:(b + 1) * P], ident[:, :])
                last.then_inc(tr_done, 1)

            def turn_gates(k):
                pe.wait_ge(ld_w, 16 * 8)
                for i in range(4):
                    last = nc.tensor.transpose(w_banks[k][:, i * P:(i + 1) * P], w_raw[:, 4 * k + i, :], ident[:, :])
                last.then_inc(gw_tr, 1)

            turn_x(0)
            turn_x(1)
            pe.wait_ge(xl_done, 1)
            pe.wait_ge(wl_done, 1)
            for tb in range(TB):
                project_v(0, tb, XH[:, 0, :], XL[:, 0, :], first_v[tb])
            pe.wait_ge(bias_col, 1)
            for s in range(2):
                wait(pe, v_evac, 2 * s)
                pe.wait_ge(wl_done, 2)
                project(0, s, 0, q_done, first_q[s])
                pe.wait_ge(wl_done, 3)
                project(0, s, DIM, k_done, first_k[s])
            for n in range(2, 6):
                turn_x(n)
                if n == 4:
                    pe.wait_ge(ld_wo, 16)
                    pe.wait_ge(q_evac, 2)
                    for c in range(PAIRS):
                        last = nc.tensor.matmul(st[:, 0, 0, 0:1], WO[:, c, :], bcol[:, B_V + c:B_V + c + 1],
                                                start=(c == 0), stop=(c == PAIRS - 1))
                    last.then_inc(bias_fold, 1)
            for m in range(4):
                scores_for_max(0, 0, (2 * m, 2 * m + 1))
                if m < 2:
                    turn_x(6 + m)
                if m == 1:
                    pe.wait_ge(k_lo, 4)
                    turn_gates(0)
                    pe.wait_ge(bias_fin, 1)
                    turn_gates(1)
            turn_max(0, 0)
            pe.wait_ge(ones_set, 1)
            pe.wait_ge(pads_set, 6)
            pe.wait_ge(d_xs, 32)
            pe.wait_ge(bias_fin, 1)
            pe.wait_ge(xl_done, N)
            pe.wait_ge(k_lo, 4)

            def step(n, first, last):
                for s in range(PAIRS):
                    t = 8 * n + s
                    ahead = not (last and s >= 6)
                    behind = not (first and s == 0)

                    def maxima_part(j):
                        if not (last and s == 7):
                            scores_for_max(n, s + 1, (j,))

                    def out_part(c):
                        if last and s == 7:
                            pe.wait_ge(norm_done, 8 * n + c + 1)
                            project_out(mx[:, 0, :], (c,))

                    maxima_part(0)
                    if first and s == 0:
                        pe.wait_ge(k_lo, 4)
                    elif first and s == 1:
                        pe.wait_ge(t_done, 3)
                    else:
                        pe.wait_ge(den_used, t - 1)
                    if ahead:
                        project(n, s + 2, 0, q_done)
                    maxima_part(1)
                    if behind:
                        values(n, s - 1, 0)
                    if first:
                        pe.wait_ge(q_evac, t + 3)
                        if s == 0:
                            pe.wait_ge(gw_lo, 2)
                        recurrence(0, s, gate_done, s)
                    elif s == 0:
                        pe.wait_ge(q_evac, t + 3)
                        recurrence(3, n - 1, h_done, N)
                    maxima_part(2)
                    scores(n, s, 0)
                    if last and s == 7:
                        recurrence(3, N - 1, h_done, N, mx[:, 1, :])
                    out_part(0)

                    maxima_part(3)
                    if first:
                        pe.wait_ge(t_done, 3 * s + 1)
                    elif s == 0:
                        pe.wait_ge(ht_done, n)
                    elif ahead:
                        pe.wait_ge(q_evac, t + 3)
                    if ahead:
                        project(n, s + 2, DIM, k_done)
                    maxima_part(4)
                    if behind:
                        values(n, s - 1, 1)
                    maxima_part(5)
                    scores(n, s, 1)
                    if first:
                        pe.wait_ge(k_lo, 2 * t + 6)
                        recurrence(1, s, gate_done, s)
                    out_part(1)
                    out_part(2)

                    maxima_part(6)
                    if behind and first:
                        values(n, s - 1, 2)
                    if first:
                        pe.wait_ge(t_done, 3 * s + 2)
                        recurrence(2, s, gate_done, s)
                    if s == 1 and not first:
                        pe.wait_ge(k_lo, 2 * t + 6)
                        pe.wait_ge(norm_done, 8 * n)
                        project_out()
                    if behind and not first:
                        values(n, s - 1, 2)
                    maxima_part(7)
                    if first:
                        scores(n, s, 2)
                        pe.wait_ge(t_done, 3 * s + 3)
                    elif s == 1:
                        pe.wait_ge(o_evac, n)
                    elif ahead:
                        pe.wait_ge(k_lo, 2 * t + 6)
                    if s == 4 and not last:
                        pe.wait_ge(d_xs, 32 * n + 64)
                    if s < 4:
                        project_v(1, s)
                    elif not last:
                        project_v(0, s - 4)
                    if not first:
                        scores(n, s, 2)
                    out_part(3)
                    out_part(4)

                    if not (last and s == 7):
                        turn_max(n, s + 1)
                    if behind:
                        values(n, s - 1, 3)
                    if s < 4 or not last:
                        pe.wait_ge(v_evac, 4 + t + 1)
                    if behind and ahead:
                        sums(n, s - 1)
                    scores(n, s, 3)
                    if not ahead:
                        sums(n, s - 1)
                    out_part(5)
                    if s == 2 and not first:
                        pe.wait_ge(pv_evac, t)
                        turn_out(n - 1)

            batches(pe, step)
            pe.wait_ge(den_used, 8 * N - 1)
            for kb in range(TB):
                values(N - 1, 7, kb)
                for h in range(2):
                    last = nc.tensor.matmul(misc[OWN[h], :], ones[:, :], probs[:, 7 % 2, h, kb, :], start=(kb == 0),
                                            stop=(kb == TB - 1))
            last.then_inc(den_done, 1)
            pe.wait_ge(norm_done, 8 * N - 1)
            project_out(mx[:, 0, :], (PAIRS - 2,))
            pe.wait_ge(norm_done, 8 * N)
            project_out(mx[:, 0, :], (PAIRS - 1,))
            pe.wait_ge(pv_evac, 8 * N)
            turn_out(N - 1)


_INS = ['L0_attn_data', 'L0_attn_W_qkv', 'L0_attn_b_qkv', 'L0_attn_W_out', 'L0_attn_b_out', 'L0_ffn_wf', 'L0_ffn_uf',
        'L0_ffn_bf', 'L0_ffn_wi', 'L0_ffn_ui', 'L0_ffn_bi', 'L0_ffn_wc', 'L0_ffn_uc', 'L0_ffn_bc', 'L0_ffn_wo',
        'L0_ffn_uo', 'L0_ffn_bo', 'L0_ffn_in_c']


def kernel(**inputs):
    import numpy as _np
    import concourse.bacc as _bacc
    from concourse import mybir as _mybir
    from concourse.bass_utils import run_bass_kernel_spmd as _run

    nc = _bacc.Bacc("TRN2", target_bir_lowering=False, num_devices=1)
    arrays, args = {}, []
    for name in _INS:
        a = _np.ascontiguousarray(inputs[name])
        arrays[f"in_{name}_dram"] = a
        args.append(nc.dram_tensor(f"in_{name}_dram", a.shape, _mybir.dt.from_np(a.dtype), kind="ExternalInput").ap())
    shape = arrays["in_L0_attn_data_dram"].shape
    args.append(nc.dram_tensor("out_dram", shape, _mybir.dt.float32, kind="ExternalOutput").ap())
    build_block(nc, *args)
    r = _run(nc, [arrays], core_ids=[0])
    return r.results[0]["out_dram"]
```
